# Optimizing a Trainium2 kernel written in Bass

```python
import numpy as np
import jax
import jax.numpy as jnp

def _softmax(x, axis=-1):
    return jax.nn.softmax(x, axis=axis)

def _gelu(x):
    return jax.nn.gelu(x, approximate=True)

def _silu(x):
    return jax.nn.silu(x)

def _sigmoid(x):
    return jax.nn.sigmoid(x)

def _layernorm(x, axis=-1, eps=1e-05):
    m = jnp.mean(x, axis=axis, keepdims=True)
    v = jnp.var(x, axis=axis, keepdims=True)
    return (x - m) / jnp.sqrt(v + eps)

def _scatter_add(tgt, idx, src, axis=0):
    return tgt.at[idx].add(src)

def _segment_sum(src, seg, n):
    return jax.ops.segment_sum(src, seg, n)
kernel_name = 'mk_adj_preln_d2_adj_r2_4ba3f4'

def setup_inputs(seed: int=0):
    np.random.seed(seed)
    _w = jnp.asarray

    def _rec_inputs():
        import jax
        import jax.numpy as jnp
        _gk = jax.random.key(seed)
        x = -0.0005207 + 1.001 * jax.random.normal(jax.random.fold_in(_gk, 1), (4096, 128), jnp.float32)
        _a = jax.random.bernoulli(jax.random.fold_in(_gk, 2), 0.000488281, (4096, 4096))
        adj = _a.astype(jnp.int32)
        return (x, adj)
    x, adj = _rec_inputs()

    def _L0_gnn_setup():
        import jax, jax.numpy as jnp
        import numpy as np
        N, IN_DIM, OUT_DIM = (4096, 128, 128)
        NEG_INF = -1000000000.0
        key = jax.random.key(seed)
        k1, k2, k3, k4 = jax.random.split(key, 4)
        X = jax.random.normal(k1, (N, IN_DIM), dtype=jnp.float32)
        A = jax.random.randint(k2, (N, N), 0, 2).astype(jnp.int32)
        W_fc = jax.random.normal(k3, (IN_DIM, OUT_DIM), dtype=jnp.float32) * (1.0 / np.sqrt(IN_DIM))
        b_fc = jnp.zeros((OUT_DIM,), dtype=jnp.float32)
        w_att = jax.random.normal(k4, (2 * OUT_DIM,), dtype=jnp.float32) * (1.0 / np.sqrt(2 * OUT_DIM))
        b_att = jnp.zeros((), dtype=jnp.float32)
        return {'X': X, 'A': A, 'W_fc': W_fc, 'b_fc': b_fc, 'w_att': w_att, 'b_att': b_att}
    _L0_gnn_all = _L0_gnn_setup()
    _L0_gnn_in = {k: v for k, v in _L0_gnn_all.items() if k in ('W_fc', 'b_fc', 'w_att', 'b_att')}
    del _L0_gnn_all

    def _L1_gnn_setup():
        import jax, jax.numpy as jnp
        import numpy as np
        NUM_HEADS = 4
        ALPHA = 0.2
        NEG_INF = -9000000000000000.0
        LN_EPS = 1e-05
        key = jax.random.key(seed)
        k_x, k_adj, k_W, k_a, k_g, k_b = jax.random.split(key, 6)
        N, Fin, Fout = (2048, 128, 128)
        head_dim = Fout // NUM_HEADS
        x = jax.random.normal(k_x, (N, Fin), dtype=jnp.float32)
        adj = jax.random.randint(k_adj, (N, N), 0, 2, dtype=jnp.int32)
        lim_W = 1.414 * np.sqrt(6.0 / (Fin + Fout))
        W = jax.random.uniform(k_W, (Fin, Fout), jnp.float32, -lim_W, lim_W)
        lim_a = 1.414 * np.sqrt(6.0 / (2 * head_dim + 1))
        a = jax.random.uniform(k_a, (2 * head_dim, 1), jnp.float32, -lim_a, lim_a)
        gamma = jax.random.normal(k_g, (Fout,), dtype=jnp.float32) * 0.1 + 1.0
        beta = jax.random.normal(k_b, (Fout,), dtype=jnp.float32) * 0.1
        return {'x': x, 'adj': adj, 'W': W, 'a': a, 'gamma': gamma, 'beta': beta}
    _L1_gnn_all = _L1_gnn_setup()
    _L1_gnn_in = {k: v for k, v in _L1_gnn_all.items() if k in ('W', 'a', 'gamma', 'beta')}
    del _L1_gnn_all
    return {'x': x, 'adj': adj, 'L0_gnn_W_fc': _L0_gnn_in['W_fc'], 'L0_gnn_b_fc': _L0_gnn_in['b_fc'], 'L0_gnn_w_att': _L0_gnn_in['w_att'], 'L0_gnn_b_att': _L0_gnn_in['b_att'], 'L1_gnn_W': _L1_gnn_in['W'], 'L1_gnn_a': _L1_gnn_in['a'], 'L1_gnn_gamma': _L1_gnn_in['gamma'], 'L1_gnn_beta': _L1_gnn_in['beta']}

def reference(x, adj, L0_gnn_W_fc, L0_gnn_b_fc, L0_gnn_w_att, L0_gnn_b_att, L1_gnn_W, L1_gnn_a, L1_gnn_gamma, L1_gnn_beta):
    import jax
    import jax.numpy as jnp

    def _L0_gnn_ref(X, A, W_fc, b_fc, w_att, b_att):
        import jax, jax.numpy as jnp
        import numpy as np
        N, IN_DIM, OUT_DIM = (4096, 128, 128)
        NEG_INF = -1000000000.0
        H = X @ W_fc + b_fc
        d = H.shape[1]
        s_src = H @ w_att[:d]
        s_dst = H @ w_att[d:]
        scores = s_src[:, None] + s_dst[None, :] + b_att
        scores = jnp.where(A > 0, scores, jnp.float32(NEG_INF))
        alpha = jax.nn.softmax(scores, axis=1)
        return alpha @ H

    def _L1_gnn_ref(x, adj, W, a, gamma, beta):
        import jax, jax.numpy as jnp
        import numpy as np
        NUM_HEADS = 4
        ALPHA = 0.2
        NEG_INF = -9000000000000000.0
        LN_EPS = 1e-05
        N = x.shape[0]
        H = NUM_HEADS
        D = W.shape[1] // H
        h = (x @ W).reshape(N, H, D)
        a1, a2 = (a[:D, 0], a[D:, 0])
        si = jnp.einsum('nhd,d->nh', h, a1)
        sj = jnp.einsum('nhd,d->nh', h, a2)
        e = si[:, :, None] + sj.T[None, :, :]
        e = jnp.where(e > 0, e, ALPHA * e)
        mask = adj[:, None, :] > 0
        e = jnp.where(mask, e, NEG_INF)
        attn = jax.nn.softmax(e, axis=-1)
        out = jnp.einsum('nhm,mhd->nhd', attn, h).reshape(N, H * D)
        mu = out.mean(axis=-1, keepdims=True)
        var = out.var(axis=-1, keepdims=True)
        return gamma * (out - mu) * jax.lax.rsqrt(var + LN_EPS) + beta
    h = jnp.maximum(_layernorm(x, axis=-1), 0.0)
    x = x + _L0_gnn_ref(h, adj, L0_gnn_W_fc, L0_gnn_b_fc, L0_gnn_w_att, L0_gnn_b_att)
    h = jnp.maximum(_layernorm(x, axis=-1), 0.0)
    x = x + _L1_gnn_ref(h, adj, L1_gnn_W, L1_gnn_a, L1_gnn_gamma, L1_gnn_beta)
    return x

_drawn_inputs = setup_inputs


def setup_inputs(seed=0):
    import zlib

    import numpy as np

    out = dict(_drawn_inputs(seed))
    spreads = {'L0_gnn_b_fc': (0.0, 0.1)}
    factors = {}
    for name, (base, spread) in spreads.items():
        noise = np.random.default_rng([zlib.crc32(name.encode()), seed]).standard_normal(out[name].shape)
        drawn = base * np.exp(spread * noise) if base else spread * noise
        out[name] = jnp.asarray(drawn.astype(out[name].dtype))
    for name, factor in factors.items():
        out[name] = (out[name] * factor).astype(out[name].dtype)
    return out
```

```python
import concourse.bass as bass
from concourse import mybir
from contextlib import ExitStack



def gnn_two_layers(nc, x, adj, w_fc, b_fc, w_att, b_att, w1, a1, gamma, beta, out):
    f32 = mybir.dt.float32
    bf16 = mybir.dt.bfloat16
    f16 = mybir.dt.float16
    f8 = mybir.dt.float8e4
    i32 = mybir.dt.int32
    u32 = mybir.dt.uint32
    u16 = mybir.dt.uint16
    i8 = mybir.dt.int8
    u8 = mybir.dt.uint8
    ALU = mybir.AluOpType
    ACT = mybir.ActivationFunctionType
    AX = mybir.AxisListType.X

    N, D = x.shape
    P = 128
    NB = N // P
    NT = NB // 2
    HEADS = 4
    DH = D // HEADS
    C0 = D + 1
    W0 = 3 * C0 + 1
    C1 = DH + 1
    W1 = 3 * C1
    E0, E1 = D + 2, D + 2 * HEADS
    HALF = N // 2
    GB = NB // 2
    EPS = 1e-5
    SLOPE = 0.2
    ONE = 56
    BANK = 512

    x_v = x.rearrange("(t m p) d -> m t (p d)", m=P, p=2)
    out_v = out.rearrange("(t m p) d -> m t (p d)", m=P, p=2)
    adj_v = adj.rearrange("(t m p) j -> t p m j", m=P, p=2)
    x1_dram = nc.dram_tensor("x1_rows", (P, NT, 2 * D), f32, kind="Internal").ap()
    si_dram = nc.dram_tensor("si_rows", (HEADS * NB, P), f32, kind="Internal").ap()

    ctx = ExitStack()
    with ctx:
        def sb(name, shape, dt):
            return ctx.enter_context(nc.sbuf_tensor(name, shape, dt))

        def sem(name):
            return ctx.enter_context(nc.semaphore(name))

        def part(arena, at, shape, dt):
            size = mybir.dt.size(dt)
            n = size
            for k in shape:
                n *= k
            v = arena[:, at:at + n].bitcast(dt)
            if len(shape) == 2:
                v = v.rearrange("p (a b) -> p a b", b=shape[1])
            if len(shape) == 3:
                v = v.rearrange("p (a b c) -> p a b c", b=shape[1], c=shape[2])
            if len(shape) == 4:
                v = v.rearrange("p (a b c d) -> p a b c d", b=shape[1], c=shape[2], d=shape[3])
            return v

        adjT = sb("adjT", [P, NT * N], u16)
        adj_word = adjT[:, :].rearrange("p (t i) -> p t i", i=N)
        adj_u32 = adjT[:, :].bitcast(u32).rearrange("p (t i) -> p t i", i=N // 2)
        adj_f8 = adjT[:, :].bitcast(f8).rearrange("p (t i b) -> p t i b", i=N, b=2)

        hx = sb("hx", [P, NB, E1], f32)

        arena_a = sb("arena_a", [P, 40960], u8)
        stage = [part(arena_a, q * 8192, [HALF], i32) for q in range(4)]
        mask = [part(arena_a, 32768 + q * 2048, [HALF], u8) for q in range(2)]
        words = [part(arena_a, 36864 + q * 2048, [HALF // 2], f16) for q in range(2)]
        srow = [part(arena_a, g * 8192, [HALF], f32) for g in range(2)]
        cmp_i8 = [part(arena_a, 16384 + k * 4096, [HALF, 2], i8) for k in range(2)]
        cmp_u32 = [part(arena_a, 16384 + k * 4096, [HALF // 2], u32) for k in range(2)]
        q_u32 = [[part(arena_a, 24576 + (2 * k + b) * 4096, [HALF // 2], u32) for b in range(2)]
                 for k in range(2)]
        q_f8 = [[part(arena_a, 24576 + (2 * k + b) * 4096, [HALF, 2], f8) for b in range(2)]
                for k in range(2)]

        arena_b = sb("arena_b", [P, NB * W0 * 2], u8)
        v0 = part(arena_b, 0, [NB, W0], bf16)
        v0_parts = v0[:, :, 0:3 * C0].rearrange("p j (c s) -> p j c s", s=3)
        xin = part(arena_b, 0, [NB, D], f32)
        wt = part(arena_b, 16384, [2, D], f32)
        wa0 = part(arena_b, 17408, [2], f32)
        wa1 = part(arena_b, 17416, [2 * HEADS], f32)
        bcol = part(arena_b, 17448, [1], f32)
        raw0 = part(arena_b, 18432, [NB, 6], f32)
        bcol_wide = part(arena_b, 17456, [P], f32)
        v1 = part(arena_b, 0, [NB, 2, W1], bf16)
        v1_bytes = NB * 2 * W1 * 2
        res = [part(arena_b, v1_bytes + g * GB * 2 * C1 * 4, [GB, 2, C1], f32) for g in range(2)]
        tot = part(arena_b, v1_bytes + 2 * GB * 2 * C1 * 4, [GB, C1], f32)
        at_b = v1_bytes + 2 * GB * 2 * C1 * 4 + GB * C1 * 4
        prod_pool = part(arena_b, at_b, [4, 2, C1], f32)

        arena_c = sb("arena_c", [P, GB * C1 * 4], u8)
        xb = part(arena_c, 0, [2, 2, D], f32)
        tmp = part(arena_c, 0, [GB, C1], f32)

        arena_d = sb("arena_d", [P, 2 * E0 * 4], u8)
        wx0 = part(arena_d, 0, [E0], f32)
        bias0 = part(arena_d, E0 * 4, [E0], f32)
        ac = part(arena_d, 0, [HEADS, 2, NB], f32)

        ident = sb("ident", [P, P], f32)
        ident_h = sb("ident_h", [P, P], f16)
        ones = sb("ones", [P, P], f32)
        wx1 = sb("wx1", [P, E1], f32)
        hsum0 = sb("hsum0", [P, D], f32)
        hsum1 = sb("hsum1", [P, HEADS, C1], f32)
        gam = sb("gam", [P, D], f32)
        bet = sb("bet", [P, D], f32)
        agg = sb("agg", [P, 2, C0], f32)
        cent = sb("cent", [P, 2, D], f32)
        hT = sb("hT", [P, 2, D], f32)
        stats = sb("stats", [P, 2, 6], f32)
        mv = sb("mv", [P, NB, 2], f32)
        std = sb("std", [P, NB], f32)
        rstd = sb("rstd", [P, NB], f32)
        bd = sb("bd", [P, HEADS, NB, 2], f32)
        nsj = sb("nsj", [P, HEADS, NB], f32)
        lone = sb("lone", [P, NB], f32)
        fac = sb("fac", [P, NB], f32)
        wj = sb("wj", [P, NB], f32)
        small = sb("small", [P, 16], f32)
        eps = sb("eps", [P, 1], f32)
        max_neg = sb("max_neg", [P, 1], f32)
        max4 = sb("max4", [P, HEADS], f32)
        diag4 = sb("diag4", [HEADS, HEADS], f32)
        batt = sb("batt", [P, 1], f32)
        t_a = cent[:, 0, :].rearrange("p (h b) -> p h b", b=NB)
        t_b = cent[:, 1, :].rearrange("p (h b) -> p h b", b=NB)
        t_c = hT[:, 0, :].rearrange("p (h b) -> p h b", b=NB)
        siT = hT[:, 1, :]
        den = hT[:, 1, :].rearrange("p (h b) -> p h b", b=NB)
        si_flat = agg[:, :, :].rearrange("p k c -> p (k c)")[:, 0:HEADS * NB]

        ps = ctx.enter_context(nc.psum_tensor("ps", [P, 8 * BANK], f32))
        ps_words = [ps[:, k * BANK:(k + 1) * BANK].bitcast(f16) for k in range(2)]
        ps_l0 = [[ps[:, (2 + 2 * u + k) * BANK:(2 + 2 * u + k) * BANK + W0] for k in range(2)]
                 for u in range(2)]
        ps_l0_pair = [ps[:, (2 + 2 * u) * BANK:(4 + 2 * u) * BANK].rearrange("p (k c) -> p k c", k=2)
                      for u in range(2)]
        ps_t = ps[:, 6 * BANK:6 * BANK + 2 * D].rearrange("p (k c) -> p k c", k=2)
        ps_p = ps[:, 7 * BANK:7 * BANK + 2 * E1].rearrange("p (k c) -> p k c", k=2)
        ps_acc = ps[:, :].rearrange("p (b c) -> p b c", c=BANK)

        waits_passed = sem("waits_passed")
        x_in = sem("x_in")
        w_in = sem("w_in")
        wa1_zero = sem("wa1_zero")
        zeros = sem("zeros")
        consts = sem("consts")
        adj_in = [sem(f"adj_in{q}") for q in range(4)]
        xb_in = [sem(f"xb_in{u}") for u in range(2)]
        x1_stored = [sem(f"x1_stored{u}") for u in range(2)]
        stats_made = sem("stats_made")
        aggr_made = sem("aggr_made")
        bcol_made = sem("bcol_made")
        w_T = sem("w_T")
        wt_made = sem("wt_made")
        wx_done = sem("wx_done")
        wx_made = sem("wx_made")
        std0_made = sem("std0_made")
        rstd0_made = sem("rstd0_made")
        h0_made = sem("h0_made")
        hsum_done = sem("hsum_done")
        hsum_read = sem("hsum_read")
        max_part = sem("max_part")
        max_row = sem("max_row")
        max_one = sem("max_one")
        max_all = sem("max_all")
        neg_made = sem("neg_made")
        fac_steps = sem("fac_steps")
        fac_made = sem("fac_made")
        wj_made = sem("wj_made")
        one_made = sem("one_made")
        v0_rest = sem("v0_rest")
        v0_cast = sem("v0_cast")
        masked = sem("masked")
        packed = sem("packed")
        transposed = sem("transposed")
        adj_kept = sem("adj_kept")
        l0_done = sem("l0_done")
        l0_read = sem("l0_read")
        epi = sem("epi")
        x1_made = sem("x1_made")
        mv_made = sem("mv_made")
        std_made = sem("std_made")
        rstd_made = sem("rstd_made")
        cent_made = sem("cent_made")
        cent_T = sem("cent_T")
        hT_made = sem("hT_made")
        proj_done = sem("proj_done")
        h1_made = sem("h1_made")
        tr_max = sem("tr_max")
        tr_diag = sem("tr_diag")
        tr_pe = sem("tr_pe")
        tr_steps = sem("tr_steps")
        bexp_in = sem("bexp_in")
        aexp_in = sem("aexp_in")
        si_flat_made = sem("si_flat_made")
        si_T = sem("si_T")
        exps_made = sem("exps_made")
        siT_made = sem("siT_made")
        hsum1_done = sem("hsum1_done")
        si_out = sem("si_out")
        srow_in = [sem(f"srow_in{g}") for g in range(2)]
        cmp_act = sem("cmp_act")
        cmp_dve = sem("cmp_dve")
        q_made = sem("q_made")
        rest_made = sem("rest_made")
        pv_done = sem("pv_done")
        bank_done = sem("bank_done")
        bank_read = sem("bank_read")
        v1_made = sem("v1_made")
        v1_chain = sem("v1_chain")
        fin_chain = sem("fin_chain")
        head_out = sem("head_out")
        o_rden = sem("o_rden")
        o_scaled = sem("o_scaled")
        o_stats = sem("o_stats")
        o_aggr = sem("o_aggr")
        o_std = sem("o_std")
        o_rstd = sem("o_rstd")
        o_bias_made = sem("o_bias_made")
        o_x1 = [sem(f"o_x1_{k}") for k in range(2)]
        o_xbeta = sem("o_xbeta")
        o_norm = sem("o_norm")
        o_gam = sem("o_gam")
        o_made = sem("o_made")
        o_out = [sem(f"o_out{k}") for k in range(2)]

        NU = NT
        BANKS = 8
        EPI = 7
        V1_LINKS = 6
        CH = 4
        NCH = NB // CH
        OG = 4
        NOG = NB // OG
        V0_STEPS = [(c, s) for k in range(NCH + 2) for s in range(3) for c in [k - s] if 0 <= c < NCH]
        V0_COUNT = {cs: n + 1 for n, cs in enumerate(V0_STEPS)}
        o_x1_buf = [part(arena_a, k * 2048, [OG, D], f32) for k in range(2)]
        o_y_buf = [part(arena_a, 4096 + k * 2048, [OG, D], f32) for k in range(2)]
        o_bias = part(arena_a, 8192, [NB], f32)
        o_raw = part(arena_a, 8704, [NB, 6], f32)

        def flat(ap):
            return ap.rearrange("p a c -> p (a c)")

        def row(t3, b, cols=None):
            v = t3[:, bass.ds(b, 1), :] if cols is None else t3[:, bass.ds(b, 1), cols]
            return flat(v)

        def wait_value(eng, signal, value):
            eng.wait_ge(signal, value).then_inc(waits_passed, 1)

        def mean_variance(dve, raw, done):
            even, odd = raw[:, :, 1], raw[:, :, 4]
            total, gap, gap2 = [cent[:, 0, n * NB:(n + 1) * NB] for n in range(3)]
            nc.vector.tensor_tensor(gap, even, odd, ALU.subtract).then_inc(done, 1)
            nc.vector.tensor_tensor(total, even, odd, ALU.add).then_inc(done, 1)
            nc.vector.tensor_tensor(mv[:, :, 1], raw[:, :, 2], raw[:, :, 5], ALU.add).then_inc(done, 1)
            dve.wait_ge(done, 3)
            nc.vector.tensor_scalar(mv[:, :, 0], total, 0.5, None, ALU.mult).then_inc(done, 1)
            nc.vector.tensor_tensor(gap2, gap, gap, ALU.mult).then_inc(done, 1)
            nc.vector.tensor_scalar(mv[:, :, 1], mv[:, :, 1], 1.0 / D, None, ALU.mult).then_inc(done, 1)
            dve.wait_ge(done, 6)
            nc.vector.scalar_tensor_tensor(out=mv[:, :, 1], in0=gap2, scalar=0.25, in1=mv[:, :, 1],
                                           op0=ALU.mult, op1=ALU.add).then_inc(done, 1)

        block = ctx.enter_context(nc.Block())

        @block.sync
        def _(sp):
            sp.dma_start(xin.rearrange("p (t q) d -> p t (q d)", q=2), x_v).then_inc(x_in, 16)

            def body(t, u, has0, has1, has2, half):
                if has0:
                    for q in range(4):
                        if not isinstance(t, int) or t > 0:
                            sp.wait_ge(masked, t * 4 + q - 3)
                        sp.dma_start(stage[q], adj_v[t, q // 2][:, (q % 2) * HALF:(q % 2 + 1) * HALF])\
                          .then_inc(adj_in[q], 16)
                if has1:
                    v = 1 - u
                    if not isinstance(t, int) or t > 2:
                        wait_value(sp, x1_stored[v], (half if u else half - 1) * 16)
                        sp.wait_ge(cent_made, t + NT - 2)
                    sp.dma_start(flat(xb[:, v]), x_v[:, t - 1]).then_inc(xb_in[v], 16)
                if has2:
                    sp.wait_ge(x1_made, t - 1)
                    sp.dma_start(x1_dram[:, t - 2], flat(xb[:, u])).then_inc(x1_stored[u], 16)

            body(0, 0, True, False, False, 0)
            body(1, 1, True, True, False, 0)
            body(2, 0, True, True, True, 1)
            body(3, 1, True, True, True, 1)
            with sp.Fori(2, NT // 2) as half:
                body(half * 2, 0, True, True, True, half)
                body(half * 2 + 1, 1, True, True, True, half)
            body(NT, 0, False, True, True, NT // 2)
            body(NT + 1, 1, False, False, True, NT // 2)

            sp.wait_ge(siT_made, 1)
            sp.dma_start(si_dram, siT).then_inc(si_out, 16)
            sp.wait_ge(si_out, 16)
            si_v = si_dram.rearrange("(h g b) m -> h g (b m)", h=HEADS, g=2)

            def rows(h, g):
                sp.dma_start(srow[g], si_v[h, g].partition_broadcast(P)).then_inc(srow_in[g], 16)

            rows(0, 0)
            rows(0, 1)
            with sp.Fori(1, HEADS) as h:
                for g in range(2):
                    wait_value(sp, cmp_act, h * (2 * NU) + (g + 1 - 2) * NU)
                    wait_value(sp, q_made, h * (2 * NU) + (g + 1 - 2) * NU + 2)
                    rows(h, g)

            def x1_load(n, k):
                sp.dma_start(o_x1_buf[k].rearrange("p (t q) d -> p t (q d)", q=2),
                             x1_dram[:, n * (OG // 2):(n + 1) * (OG // 2)]).then_inc(o_x1[k], 16)

            for u in range(2):
                sp.wait_ge(x1_stored[u], 16 * (NT // 2))
            sp.wait_ge(head_out, 2 * HEADS + 2)
            x1_load(0, 0)
            x1_load(1, 1)
            for n in range(NOG):
                k = n % 2
                sp.wait_ge(o_made, n + 1)
                sp.dma_start(out_v[:, n * (OG // 2):(n + 1) * (OG // 2)],
                             o_y_buf[k].rearrange("p (t q) d -> p t (q d)", q=2)).then_inc(o_out[k], 16)
                if n + 2 < NOG:
                    x1_load(n + 2, k)
            for k in range(2):
                sp.wait_ge(o_out[k], 16 * (NOG // 2))

        @block.gpsimd
        def _(pool):
            nc.gpsimd.memset(wa1, 0.0).then_inc(wa1_zero, 1)
            nc.gpsimd.memset(ident[:, :], 0.0).then_inc(zeros, 1)
            nc.gpsimd.memset(ident_h[:, :], 0.0).then_inc(zeros, 1)
            nc.gpsimd.memset(ones[:, :], 1.0).then_inc(consts, 1)
            nc.gpsimd.memset(eps[:, :], EPS).then_inc(consts, 1)
            nc.gpsimd.memset(hsum1[:, :, DH:C1], float(N)).then_inc(head_out, 2)
            pool.wait_ge(zeros, 2)
            for m in (ident, ident_h):
                nc.gpsimd.affine_select(out=m[:, :], in_=m[:, :], compare_op=ALU.not_equal, fill=1.0,
                                        base=0, pattern=[[-1, P]], channel_multiplier=1).then_inc(consts, 1)

            def build(h, c):
                js = slice(c * CH, (c + 1) * CH)
                dst = v1[:, js].rearrange("p j b (c s) -> p (j b) c s", s=3)
                prod = prod_pool.rearrange("p j b c -> p (j b) c")
                base = h * (NCH * V1_LINKS) + c * V1_LINKS

                def link(ins, k):
                    ins.then_inc(v1_chain, 1)
                    wait_value(pool, v1_chain, base + k)

                if not isinstance(h, int) or c > 0:
                    wait_value(pool, v1_made, h * NCH + c)
                bd_h = bd[:, bass.ds(h, 1), js, :].rearrange("p a j b -> p (a j) b")
                nc.gpsimd.tensor_copy(prod_pool[:, :, :, DH], bd_h)
                for b in range(2):
                    last = nc.gpsimd.tensor_tensor(prod_pool[:, :, b, 0:DH], hx[:, js, bass.ds(h * DH, DH)],
                                                   bd_h[:, :, b].unsqueeze(2).to_broadcast([P, CH, DH]),
                                                   ALU.mult)
                    link(last, b + 1)
                link(nc.gpsimd.tensor_copy(dst[:, :, :, 0], prod), 3)
                link(nc.gpsimd.tensor_tensor(prod, prod, dst[:, :, :, 0], ALU.subtract), 4)
                link(nc.gpsimd.tensor_copy(dst[:, :, :, 1], prod), 5)
                link(nc.gpsimd.tensor_tensor(prod, prod, dst[:, :, :, 1], ALU.subtract), 6)
                nc.gpsimd.tensor_copy(dst[:, :, :, 2], prod).then_inc(v1_made, 1)

            FIN = 4

            def finish(h, g):
                blk = slice(g * GB, (g + 1) * GB)

                def link(ins, k):
                    ins.then_inc(fin_chain, 1)
                    wait_value(pool, fin_chain, (h * 2 + g) * FIN + k)

                def factor(k):
                    return ac[:, bass.ds(h, 1), k, blk].rearrange("p a b -> p (a b)").unsqueeze(2)\
                        .to_broadcast([P, GB, C1])

                wait_value(pool, bank_read, (h * 2 + g + 2) * BANKS)
                wait_value(pool, head_out, h * 2 + g + 2)
                nc.gpsimd.tensor_tensor(tot, res[g][:, :, 0, :], factor(0), ALU.mult)
                link(nc.gpsimd.tensor_tensor(tmp, res[g][:, :, 1, :], factor(1), ALU.mult), 1)
                link(nc.gpsimd.tensor_tensor(tot, tot, tmp, ALU.add), 2)
                link(nc.gpsimd.tensor_tensor(tmp, lone[:, blk].unsqueeze(2).to_broadcast([P, GB, C1]),
                                             hsum1[:, bass.ds(h, 1), :].to_broadcast([P, GB, C1]),
                                             ALU.mult), 3)
                link(nc.gpsimd.tensor_tensor(tot, tot, tmp, ALU.add), 4)
                nc.gpsimd.tensor_copy(den[:, bass.ds(h, 1), blk].rearrange("p a b -> p (a b)"), tot[:, :, DH])
                nc.gpsimd.tensor_copy(hx[:, blk, bass.ds(h * DH, DH)], tot[:, :, 0:DH]).then_inc(head_out, 1)

            pool.wait_ge(exps_made, 4)
            for c in range(NCH):
                build(0, c)
            pool.wait_ge(head_out, 2)
            with pool.Fori(0, HEADS - 1) as h:
                finish(h, 0)
                for c in range(NCH):
                    wait_value(pool, pv_done, h * (2 * NU) + NU + (c + 1) * (CH // 2) + 2)
                    build(h + 1, c)
                finish(h, 1)
            finish(HEADS - 1, 0)
            finish(HEADS - 1, 1)

            for n in range(NOG):
                k = n % 2
                pool.wait_ge(o_x1[k], 16 * (n // 2 + 1))
                nc.gpsimd.tensor_tensor(o_x1_buf[k], o_x1_buf[k],
                                        bet[:, :].unsqueeze(1).to_broadcast([P, OG, D]), ALU.add)\
                    .then_inc(o_xbeta, 1)

        @block.scalar
        def _(act):
            act.dma_start(wx0[:, 0:D], w_fc).then_inc(w_in, 16)
            act.dma_start(wx1[:, 0:D], w1).then_inc(w_in, 16)
            for k in range(2):
                act.dma_start(wa0[:, k:k + 1], w_att[k * D:(k + 1) * D].rearrange("(n a) -> n a", a=1))\
                   .then_inc(w_in, 16)
            act.dma_start(bcol, b_fc.rearrange("(n a) -> n a", a=1)).then_inc(w_in, 16)
            act.dma_start(batt[:, :], b_att.partition_broadcast(P)).then_inc(w_in, 16)
            act.dma_start(gam[:, :], gamma.partition_broadcast(P)).then_inc(w_in, 16)
            act.dma_start(bet[:, :], beta.partition_broadcast(P)).then_inc(w_in, 16)
            act.wait_ge(wa1_zero, 1)
            for h in range(HEADS):
                for k in range(2):
                    act.dma_start(wa1[h * DH:(h + 1) * DH, k * HEADS + h:k * HEADS + h + 1],
                                  a1[k * DH:(k + 1) * DH, :]).then_inc(w_in, 16)

            act.wait_ge(aggr_made, 7)
            act.wait_ge(consts, 4)
            nc.scalar.activation(std[:, :], mv[:, :, 1], ACT.Sqrt, bias=eps[:, :]).then_inc(std0_made, 1)
            act.wait_ge(cent_T, 1)
            nc.scalar.activation(hT[:, :, :], ps_t, ACT.Copy).then_inc(hT_made, 1)
            with act.Fori(1, NT) as t:
                act.wait_ge(cent_T, t + 1)
                act.wait_ge(proj_done, t)
                nc.scalar.activation(hT[:, :, :], ps_t, ACT.Copy).then_inc(hT_made, 1)
            act.wait_ge(neg_made, 1)
            nc.scalar.activation(wj[:, :], hx[:, :, D + 1], ACT.Exp, bias=max_neg[:, :]).then_inc(wj_made, 1)
            act.wait_ge(fac_made, 1)
            nc.scalar.activation(fac[:, :], fac[:, :], ACT.Exp).then_inc(wj_made, 1)
            for c, s in V0_STEPS:
                js = slice(c * CH, (c + 1) * CH)
                act.wait_ge(v0_rest, V0_COUNT[c, s])
                nc.scalar.activation(v0_parts[:, js, :, s], hx[:, js, 0:C0], ACT.Copy).then_inc(v0_cast, 1)

            def body(t, has0, has1, has2):
                def keep(q):
                    act.wait_ge(transposed, t * 4 + q + 1)
                    nc.scalar.activation(
                        adj_word[:, (q % 2) * (NT // 2):(q % 2 + 1) * (NT // 2),
                                 bass.ds(t * (2 * P) + (q // 2) * P, P)],
                        ps_words[q % 2].rearrange("p (a m) -> p a m", m=P), ACT.Copy,
                        scale=float(ONE)).then_inc(adj_kept, 1)
                if has0:
                    keep(0)
                    keep(1)
                if has2:
                    act.wait_ge(cent_T, t + NT - 1)
                    nc.scalar.activation(hT[:, :, :], ps_t, ACT.Copy).then_inc(hT_made, 1)
                    act.wait_ge(proj_done, t + NT - 1)
                    act.wait_ge(rstd_made, t - 1)
                    for k in range(2):
                        nc.scalar.activation(row(hx, t * 2 - 4 + k), ps_p[:, k, :], ACT.Copy,
                                             scale=rstd[:, k:k + 1]).then_inc(h1_made, 1)
                if has0:
                    keep(2)
                    keep(3)
                if has1:
                    act.wait_ge(mv_made, t)
                    nc.scalar.activation(std[:, 0:2], mv[:, 0:2, 1], ACT.Sqrt, bias=eps[:, :])\
                        .then_inc(std_made, 1)

            body(0, True, False, False)
            body(1, True, True, False)
            with act.Fori(2, NT) as t:
                body(t, True, True, True)
            body(NT, False, True, True)
            body(NT + 1, False, False, True)

            act.wait_ge(bexp_in, 1)
            for k, slope in enumerate((1.0, SLOPE)):
                nc.scalar.activation(bd[:, :, :, k], t_a, ACT.Exp, scale=slope).then_inc(exps_made, 1)
            act.wait_ge(aexp_in, 2)
            for k, t_k in enumerate((t_b, t_c)):
                nc.scalar.activation(ac[:, :, k, :], t_k, ACT.Exp).then_inc(exps_made, 1)
            act.wait_ge(si_T, 1)
            nc.scalar.activation(siT, ps[:, 2 * BANK:2 * BANK + P], ACT.Copy).then_inc(siT_made, 1)

            with act.Fori(0, HEADS) as h:
                for g in range(2):
                    wait_value(act, srow_in[g], h * 16 + 16)
                    with act.Fori(0, NU // 2) as jj:
                        for k in range(2):
                            act.wait_ge(q_made, h * (2 * NU) + g * NU + jj * 2 + k + 1)
                            for p in range(k + 1):
                                last = nc.scalar.activation(
                                    cmp_i8[k][:, :, p], srow[g], ACT.Sign, scale=-1.0,
                                    bias=row(nsj, h, bass.ds(jj * 4 + 2 * k + p, 1)))
                            last.then_inc(cmp_act, 1)

            act.wait_ge(o_aggr, 7)
            nc.scalar.activation(std[:, :], mv[:, :, 1], ACT.Sqrt, bias=eps[:, :]).then_inc(o_std, 1)
            act.wait_ge(o_bias_made, 1)
            for n in range(NOG):
                k = n % 2
                if n >= 2:
                    act.wait_ge(o_out[k], 16 * (n // 2))
                for b in range(OG):
                    B = n * OG + b
                    last = nc.scalar.activation(o_y_buf[k][:, b, :], hx[:, B, 0:D], ACT.Identity,
                                                scale=rstd[:, B:B + 1], bias=o_bias[:, B:B + 1])
                last.then_inc(o_norm, 1)

        @block.vector
        def _(dve):
            dve.wait_ge(x_in, 16)
            with dve.Fori(0, NB) as b:
                nc.vector.bn_stats(row(raw0, b), row(xin, b)).then_inc(stats_made, 1)
            dve.wait_ge(stats_made, NB)
            mean_variance(dve, raw0, aggr_made)
            dve.wait_ge(w_in, 16 * (8 + 2 * HEADS))
            dve.wait_ge(consts, 4)
            nc.vector.tensor_scalar(bcol_wide, ones[:, :], bcol, None, ALU.mult).then_inc(bcol_made, 1)
            dve.wait_ge(w_T, 1)
            nc.vector.tensor_copy(wt, ps_t).then_inc(wt_made, 1)
            dve.wait_ge(wx_done, 1)
            at = 7 * BANK
            nc.vector.tensor_copy(wx0[:, D:E0], ps[:, at:at + 2])
            nc.vector.tensor_copy(wx1[:, D:E1], ps[:, at + 2:at + 2 + 2 * HEADS])
            nc.vector.tensor_copy(bias0[:, :], ps[:, at + 16:at + 16 + E0]).then_inc(wx_made, 1)
            dve.wait_ge(std0_made, 1)
            nc.vector.reciprocal(rstd[:, :], std[:, :]).then_inc(rstd0_made, 1)
            dve.wait_ge(rstd0_made, 1)
            dve.wait_ge(wx_made, 1)

            def center(t):
                for k in range(2):
                    last = nc.vector.tensor_scalar(row(xin, t * 2 + k), row(xin, t * 2 + k),
                                                   row(mv, t * 2 + k, slice(0, 1)), 0.0,
                                                   ALU.subtract, ALU.max)
                last.then_inc(cent_made, 1)

            def scaled(t):
                dve.wait_ge(proj_done, t + 1)
                for k in range(2):
                    last = nc.vector.scalar_tensor_tensor(
                        out=row(hx, t * 2 + k, slice(0, E0)), in0=ps_p[:, k, 0:E0],
                        scalar=rstd[:, bass.ds(t * 2 + k, 1)], in1=bias0[:, :], op0=ALU.mult, op1=ALU.add)
                last.then_inc(h0_made, 1)

            center(0)
            with dve.Fori(1, NT) as t:
                center(t)
                scaled(t - 1)
            scaled(NT - 1)
            dve.wait_ge(h0_made, NT)

            nc.vector.reduce_max(small[:, 0:1], hx[:, :, D + 1], AX).then_inc(max_part, 1)
            nc.vector.tensor_scalar(fac[:, :], hx[:, :, D], batt[:, :], None, ALU.add).then_inc(fac_steps, 1)
            dve.wait_ge(max_row, 1)
            nc.vector.reduce_max(small[0:1, 2:3], ps[0:1, 6 * BANK:6 * BANK + P], AX).then_inc(max_one, 1)
            dve.wait_ge(max_all, 1)
            nc.vector.tensor_scalar(max_neg[:, :], ps[:, 7 * BANK:7 * BANK + 1], -1.0, None, ALU.mult)\
                .then_inc(neg_made, 1)
            dve.wait_ge(neg_made, 1)
            dve.wait_ge(fac_steps, 1)
            nc.vector.tensor_scalar(std[:, :], fac[:, :], max_neg[:, :], None, ALU.subtract)\
                .then_inc(fac_steps, 1)
            dve.wait_ge(fac_steps, 2)
            nc.vector.scalar_tensor_tensor(out=fac[:, :], in0=fac[:, :], scalar=max_neg[:, :],
                                           in1=std[:, :], op0=ALU.subtract, op1=ALU.subtract)\
                .then_inc(fac_made, 1)
            dve.wait_ge(hsum_done, 1)
            nc.vector.tensor_copy(hsum0[:, :], ps[:, 5 * BANK:5 * BANK + D]).then_inc(hsum_read, 1)
            nc.vector.memset(hx[:, :, D:C0], 1.0).then_inc(one_made, 1)
            nc.vector.memset(v0[:, :, W0 - 1:W0], 1.0).then_inc(one_made, 1)
            dve.wait_ge(one_made, 2)
            dve.wait_ge(wj_made, 1)
            for c, s in V0_STEPS:
                js = slice(c * CH, (c + 1) * CH)
                if s == 0:
                    nc.vector.tensor_tensor(hx[:, js, 0:C0], hx[:, js, 0:C0],
                                            wj[:, js].unsqueeze(2).to_broadcast([P, CH, C0]), ALU.mult)\
                        .then_inc(v0_rest, 1)
                else:
                    dve.wait_ge(v0_cast, V0_COUNT[c, s - 1])
                    nc.vector.tensor_tensor(hx[:, js, 0:C0], hx[:, js, 0:C0], v0_parts[:, js, :, s - 1],
                                            ALU.subtract).then_inc(v0_rest, 1)
            dve.wait_ge(wj_made, 2)

            def take(t):
                def compare(q):
                    if not isinstance(t, int) or 4 * t + q >= 2:
                        dve.wait_ge(packed, t * 4 + q - 1)
                    dve.wait_ge(adj_in[q], t * 16 + 16)
                    nc.vector.tensor_scalar(mask[q % 2], stage[q], 0.0, None, ALU.is_gt).then_inc(masked, 1)

                def pack(q):
                    dve.wait_ge(masked, t * 4 + q + 1)
                    if not isinstance(t, int) or 4 * t + q >= 2:
                        dve.wait_ge(transposed, t * 4 + q - 1)
                    pair = mask[q % 2].rearrange("p (w b) -> p w b", b=2)
                    nc.vector.scalar_tensor_tensor(out=words[q % 2], in0=pair[:, :, 1], scalar=256.0,
                                                   in1=pair[:, :, 0], op0=ALU.mult, op1=ALU.add)\
                        .then_inc(packed, 1)

                for q in (0, 2):
                    compare(q)
                    compare(q + 1)
                    pack(q)
                    pack(q + 1)

            def epilogue(s, v, half):
                def link(ins, k):
                    ins.then_inc(epi, 1)
                    dve.wait_ge(epi, s * EPI + k)

                later = not isinstance(s, int) or s > 0
                two = bass.ds(s * 2, 2)
                dve.wait_ge(l0_done, s * 2 + 2)
                link(nc.vector.tensor_reduce(
                    agg[:, :, :], ps_l0_pair[v][:, :, 0:3 * C0].rearrange("p k (c s) -> p k c s", s=3),
                    AX, ALU.add), 1)
                nc.vector.tensor_scalar(lone[:, two], ps_l0_pair[v][:, :, W0 - 1], 0.0, None, ALU.is_equal)\
                    .then_inc(l0_read, 1)
                link(nc.vector.tensor_tensor(small[:, 0:2], agg[:, :, D], fac[:, two], ALU.mult), 2)
                dve.wait_ge(l0_read, s + 1)
                link(nc.vector.scalar_tensor_tensor(out=small[:, 2:4], in0=lone[:, two], scalar=float(N),
                                                    in1=small[:, 0:2], op0=ALU.mult, op1=ALU.add), 3)
                link(nc.vector.reciprocal(small[:, 4:6], small[:, 2:4]), 4)
                nc.vector.tensor_tensor(small[:, 6:8], fac[:, two], small[:, 4:6], ALU.mult)
                link(nc.vector.tensor_tensor(small[:, 8:10], lone[:, two], small[:, 4:6], ALU.mult), 5)
                dve.wait_ge(xb_in[v], half * 16 + 16)
                for k in range(2):
                    last = nc.vector.scalar_tensor_tensor(
                        out=xb[:, v, k, :], in0=agg[:, k, 0:D], scalar=small[:, 6 + k:7 + k],
                        in1=xb[:, v, k, :], op0=ALU.mult, op1=ALU.add)
                link(last, 6)
                for k in range(2):
                    last = nc.vector.scalar_tensor_tensor(
                        out=xb[:, v, k, :], in0=hsum0[:, :], scalar=small[:, 8 + k:9 + k],
                        in1=xb[:, v, k, :], op0=ALU.mult, op1=ALU.add)
                last.then_inc(x1_made, 1)
                dve.wait_ge(x1_made, s + 1)
                for k in range(2):
                    last = nc.vector.bn_stats(stats[:, k, :], xb[:, v, k, :])
                last.then_inc(epi, 1)
                wait_value(dve, epi, s * EPI + 7)
                for k in range(2):
                    last = nc.vector.bn_aggr(mv[:, k, :], stats[:, k, :])
                last.then_inc(mv_made, 1)
                dve.wait_ge(std_made, s + 1)
                if later:
                    dve.wait_ge(h1_made, s * 2)
                nc.vector.reciprocal(rstd[:, 0:2], std[:, 0:2]).then_inc(rstd_made, 1)
                if later:
                    dve.wait_ge(cent_T, s + NT)
                for k in range(2):
                    last = nc.vector.tensor_scalar(cent[:, k, :], xb[:, v, k, :], mv[:, k, 0:1], 0.0,
                                                   ALU.subtract, ALU.max)
                last.then_inc(cent_made, 1)

            take(0)
            take(1)
            epilogue(0, 0, 0)
            with dve.Fori(1, NT // 2) as half:
                take(half * 2)
                epilogue(half * 2 - 1, 1, half - 1)
                take(half * 2 + 1)
                epilogue(half * 2, 0, half)
            epilogue(NT - 1, 1, NT // 2 - 1)

            dve.wait_ge(h1_made, 2 * NT)
            si = hx[:, :, D:D + HEADS].rearrange("p j h -> p h j")
            sj = hx[:, :, D + HEADS:E1].rearrange("p j h -> p h j")
            nc.vector.reduce_max(max4[:, :], sj, AX).then_inc(tr_max, 1)
            nc.vector.tensor_copy(si_flat.rearrange("p (h j) -> p h j", j=NB), si).then_inc(si_flat_made, 1)
            nc.vector.tensor_scalar(nsj[:, :, :], sj, -1.0, None, ALU.mult).then_inc(q_made, 2)
            dve.wait_ge(q_made, 2)
            dve.wait_ge(tr_pe, 1)
            nc.vector.reduce_max(small[0:HEADS, 0:1], ps[0:HEADS, 6 * BANK:6 * BANK + P], AX)\
                .then_inc(tr_steps, 1)
            dve.wait_ge(tr_steps, 1)
            nc.vector.tensor_scalar(diag4[:, :], ident[0:HEADS, 0:HEADS], small[0:HEADS, 0:1], None, ALU.mult)\
                .then_inc(tr_diag, 1)
            dve.wait_ge(tr_pe, 2)
            nc.vector.tensor_copy(max4[:, :], ps[:, 7 * BANK:7 * BANK + HEADS]).then_inc(tr_steps, 1)
            dve.wait_ge(tr_steps, 2)
            wide = max4[:, :].unsqueeze(2).to_broadcast([P, HEADS, NB])
            nc.vector.tensor_tensor(t_a, sj, wide, ALU.subtract).then_inc(bexp_in, 1)
            nc.vector.tensor_tensor(t_b, si, wide, ALU.add).then_inc(tr_steps, 1)
            dve.wait_ge(tr_steps, 3)
            row_max = xb[:, 0].rearrange("p k d -> p (k d)")[:, 0:HEADS * NB].rearrange("p (h j) -> p h j", j=NB)
            dve.wait_ge(x1_stored[0], 16 * (NT // 2))
            nc.vector.scalar_tensor_tensor(out=row_max, in0=t_b, scalar=SLOPE, in1=t_b, op0=ALU.mult,
                                           op1=ALU.max).then_inc(tr_steps, 1)
            dve.wait_ge(tr_steps, 4)
            nc.vector.scalar_tensor_tensor(out=t_c, in0=t_b, scalar=SLOPE, in1=row_max, op0=ALU.mult,
                                           op1=ALU.subtract).then_inc(aexp_in, 1)
            dve.wait_ge(aexp_in, 1)
            nc.vector.tensor_tensor(t_b, t_b, row_max, ALU.subtract).then_inc(aexp_in, 1)
            dve.wait_ge(hsum1_done, 1)
            nc.vector.tensor_copy(hsum1[:, :, 0:DH], ps[:, 5 * BANK:5 * BANK + D]
                                  .rearrange("p (h d) -> p h d", d=DH)).then_inc(bank_read, BANKS)

            with dve.Fori(0, HEADS) as h:
                for g in range(2):
                    wait_value(dve, srow_in[g], h * 16 + 16)
                    with dve.Fori(0, NU // 2) as jj:
                        for k in range(2):
                            done = h * (2 * NU) + g * NU + jj * 2 + k
                            if k == 0:
                                nc.vector.tensor_scalar(cmp_i8[k][:, :, 1], srow[g],
                                                        row(nsj, h, bass.ds(jj * 4 + 1, 1)), float(ONE),
                                                        ALU.is_gt, ALU.mult).then_inc(cmp_dve, 1)
                                dve.wait_ge(cmp_dve, h * NU + g * (NU // 2) + jj + 1)
                            dve.wait_ge(cmp_act, done + 1)
                            dve.wait_ge(pv_done, done + 1)
                            adj_u = adj_u32[:, bass.ds(jj * 2 + k, 1), g * (HALF // 2):(g + 1) * (HALF // 2)]
                            adj_u = flat(adj_u)
                            nc.vector.tensor_tensor(q_u32[k][0], cmp_u32[k], adj_u, ALU.bitwise_and)\
                                .then_inc(q_made, 1)
                            dve.wait_ge(q_made, done + 3)
                            nc.vector.tensor_tensor(q_u32[k][1], q_u32[k][0], adj_u, ALU.bitwise_xor)\
                                .then_inc(rest_made, 1)
                    dve.wait_ge(head_out, h * 2 + g + 1)
                    for n in range(BANKS):
                        if n < BANKS - 1:
                            dve.wait_ge(bank_done, h * (2 * BANKS - 2) + g * (BANKS - 1) + n + 1)
                        else:
                            dve.wait_ge(pv_done, h * (2 * NU) + (g + 1) * NU + 2)
                        nc.vector.tensor_reduce(
                            res[g][:, 2 * n:2 * n + 2].rearrange("p a b c -> p (a b c)"),
                            ps_acc[:, n, 0:4 * W1].rearrange("p (c s) -> p c s", s=3), AX, ALU.add)\
                            .then_inc(bank_read, 1)

            dve.wait_ge(head_out, 2 * HEADS + 2)
            nc.vector.reciprocal(den, den).then_inc(o_rden, 1)
            dve.wait_ge(o_rden, 1)
            for h in range(HEADS):
                cols = hx[:, :, h * DH:(h + 1) * DH]
                last = nc.vector.tensor_tensor(cols, cols, den[:, h, :].unsqueeze(2)
                                               .to_broadcast([P, NB, DH]), ALU.mult)
            last.then_inc(o_scaled, 1)
            dve.wait_ge(o_scaled, 1)
            with dve.Fori(0, NB) as b:
                nc.vector.bn_stats(row(o_raw, b), row(hx, b, slice(0, D))).then_inc(o_stats, 1)
            dve.wait_ge(o_stats, NB)
            mean_variance(dve, o_raw, o_aggr)
            dve.wait_ge(o_std, 1)
            nc.vector.reciprocal(rstd[:, :], std[:, :]).then_inc(o_rstd, 1)
            dve.wait_ge(o_rstd, 1)
            nc.vector.scalar_tensor_tensor(out=o_bias, in0=mv[:, :, 0], scalar=-1.0, in1=rstd[:, :],
                                           op0=ALU.mult, op1=ALU.mult).then_inc(o_bias_made, 1)
            for n in range(NOG):
                k = n % 2
                dve.wait_ge(o_norm, n + 1)
                nc.vector.tensor_tensor(o_y_buf[k], o_y_buf[k],
                                        gam[:, :].unsqueeze(1).to_broadcast([P, OG, D]), ALU.mult)\
                    .then_inc(o_gam, 1)
                dve.wait_ge(o_gam, n + 1)
                dve.wait_ge(o_xbeta, n + 1)
                nc.vector.tensor_tensor(o_y_buf[k], o_y_buf[k], o_x1_buf[k], ALU.add).then_inc(o_made, 1)

        @block.tensor
        def _(pe):
            pe.wait_ge(w_in, 16 * (8 + 2 * HEADS))
            pe.wait_ge(consts, 4)
            for k, w in enumerate((wx0, wx1)):
                last = nc.tensor.transpose(ps_t[:, k, :], w[:, 0:D], ident[:, :])
            last.then_inc(w_T, 1)
            pe.wait_ge(wt_made, 1)
            pe.wait_ge(bcol_made, 1)
            at = 7 * BANK
            for o, n, lhsT, rhs in ((0, 2, wt[:, 0, :], wa0), (2, 2 * HEADS, wt[:, 1, :], wa1),
                                    (16, D, bcol_wide, ident[:, :]), (16 + D, 2, bcol_wide, wa0)):
                last = nc.tensor.matmul(ps[:, at + o:at + o + n], lhsT, rhs, start=True, stop=True)
            last.then_inc(wx_done, 1)

            def flip(t, rows_of, free):
                pe.wait_ge(cent_made, t + 1)
                if free:
                    pe.wait_ge(hT_made, t)
                for k in range(2):
                    last = nc.tensor.transpose(ps_t[:, k, :], rows_of(k), ident[:, :])
                last.then_inc(cent_T, 1)

            def project(t, w, cols):
                pe.wait_ge(hT_made, t + 1)
                for k in range(2):
                    last = nc.tensor.matmul(ps_p[:, k, 0:cols], hT[:, k, :], w[:, 0:cols], start=True, stop=True)
                last.then_inc(proj_done, 1)

            def column_sums(B):
                return nc.tensor.matmul(ps[:, 5 * BANK:5 * BANK + D], ones[:, :], hx[:, B, 0:D],
                                        start=(B == 0), stop=(B == NB - 1))

            pe.wait_ge(wx_made, 1)
            flip(0, lambda k: xin[:, k, :], False)
            for t in range(NT):
                if t + 1 < NT:
                    flip(t + 1, lambda k: xin[:, 2 * (t + 1) + k, :], True)
                if t:
                    pe.wait_ge(h0_made, t)
                project(t, wx0, E0)
                if t:
                    column_sums(2 * t - 2)
                    column_sums(2 * t - 1)
            pe.wait_ge(h0_made, NT)
            column_sums(NB - 2)
            column_sums(NB - 1).then_inc(hsum_done, 1)
            pe.wait_ge(max_part, 1)
            nc.tensor.matmul(ps[0:1, 6 * BANK:6 * BANK + P], small[:, 0:1], ident[:, :],
                             start=True, stop=True).then_inc(max_row, 1)
            pe.wait_ge(max_one, 1)
            nc.tensor.matmul(ps[:, 7 * BANK:7 * BANK + 1], ones[0:1, :], small[0:1, 2:3],
                             start=True, stop=True).then_inc(max_all, 1)

            def turn(B):
                for hf in range(2):
                    n = 2 * B + hf
                    pe.wait_ge(packed, n + 1)
                    if n >= 2:
                        pe.wait_ge(adj_kept, n - 1)
                    for a in range(NT // 2):
                        last = nc.tensor.transpose(ps_words[hf][:, a * P:(a + 1) * P],
                                                   words[hf][:, a * P:(a + 1) * P], ident_h[:, :])
                    last.then_inc(transposed, 1)

            def aggregate(B):
                s = B // 2
                pe.wait_ge(adj_kept, 2 * B + 2)
                if B % 2 == 0 and s >= 2:
                    pe.wait_ge(l0_read, s - 1)
                for J in range(NB):
                    last = nc.tensor.matmul(ps_l0[s % 2][B % 2], adj_f8[:, J // 2, B * P:(B + 1) * P, J % 2],
                                            v0[:, J, :], start=(J == 0), stop=(J == NB - 1))
                last.then_inc(l0_done, 1)

            for t in range(NT + 2):
                if t < NT:
                    turn(2 * t)
                if t == 0:
                    pe.wait_ge(v0_cast, 3 * NCH)
                    pe.wait_ge(one_made, 2)
                    pe.wait_ge(hsum_read, 1)
                if t >= 2:
                    flip(NT + t - 2, lambda k: cent[:, k, :], True)
                if 1 <= t <= NT:
                    aggregate(2 * t - 1)
                if t >= 2:
                    if t >= 3:
                        pe.wait_ge(h1_made, 2 * t - 4)
                    else:
                        pe.wait_ge(h0_made, NT)
                    project(NT + t - 2, wx1, E1)
                if t < NT:
                    turn(2 * t + 1)
                    aggregate(2 * t)

            pe.wait_ge(tr_max, 1)
            nc.tensor.matmul(ps[0:HEADS, 6 * BANK:6 * BANK + P], max4[:, :], ident[:, :],
                             start=True, stop=True).then_inc(tr_pe, 1)
            pe.wait_ge(si_flat_made, 1)
            nc.tensor.transpose(ps[:, 2 * BANK:2 * BANK + P], si_flat, ident[:, :]).then_inc(si_T, 1)
            pe.wait_ge(tr_diag, 1)
            nc.tensor.matmul(ps[:, 7 * BANK:7 * BANK + HEADS], ones[0:HEADS, :], diag4[:, :],
                             start=True, stop=True).then_inc(tr_pe, 1)
            column_sums(0).then_inc(pv_done, 2)
            for B in range(1, NB):
                last = column_sums(B)
            last.then_inc(hsum1_done, 1)

            pe.wait_ge(siT_made, 1)
            with pe.Fori(0, HEADS) as h:
                for g in range(2):
                    for jt in range(NU):
                        k = jt % 2
                        if g == 0 and jt % (CH // 2) == 0:
                            wait_value(pe, v1_made, h * NCH + jt // (CH // 2) + 1)
                        for b in range(2):
                            if b == 0:
                                wait_value(pe, q_made, h * (2 * NU) + g * NU + jt + 3)
                            else:
                                wait_value(pe, rest_made, h * (2 * NU) + g * NU + jt + 1)
                            for p in range(2):
                                for n in range(GB):
                                    bank = n // 2
                                    first = jt == 0 and b == 0 and p == 0
                                    if first and n % 2 == 0:
                                        wait_value(pe, bank_read, h * (2 * BANKS) + g * BANKS + bank + 1)
                                    at = (n % 2) * 2 * W1 + b * W1
                                    last = nc.tensor.matmul(
                                        ps_acc[:, bank, at:at + W1], q_f8[k][b][:, n * P:(n + 1) * P, p],
                                        v1[:, 2 * jt + p, b, :],
                                        start=(first and n % 2 == 0),
                                        stop=(jt == NU - 1 and b == 1 and p == 1 and n % 2 == 1),
                                        skip_group_check=True)
                                    if jt == NU - 1 and b == 1 and p == 1 and n % 2 == 1 and n < GB - 1:
                                        last.then_inc(bank_done, 1)
                        last.then_inc(pv_done, 1)


_INS = ['x', 'adj', 'L0_gnn_W_fc', 'L0_gnn_b_fc', 'L0_gnn_w_att', 'L0_gnn_b_att',
        'L1_gnn_W', 'L1_gnn_a', 'L1_gnn_gamma', 'L1_gnn_beta']
_OUTS = [((4096, 128), 'float32')]


def kernel(**inputs):
    import numpy as _np
    import concourse.bacc as _bacc
    from concourse import mybir as _mybir
    from concourse.bass_utils import run_bass_kernel_spmd as _run

    nc = _bacc.Bacc("TRN2", target_bir_lowering=False, num_devices=1, dynamic_dma_scratch_size=2048)
    arrays, args = {}, []
    for name in _INS:
        a = _np.ascontiguousarray(inputs[name])
        if name == 'L0_gnn_b_att':
            a = a.reshape(1)
        arrays[f"in_{name}_dram"] = a
        args.append(nc.dram_tensor(f"in_{name}_dram", a.shape, _mybir.dt.from_np(a.dtype), kind="ExternalInput").ap())
    for i, (shape, dtype) in enumerate(_OUTS):
        dt = _mybir.dt.from_np(_np.dtype(dtype))
        args.append(nc.dram_tensor(f"out_{i}_dram", shape, dt, kind="ExternalOutput").ap())
    gnn_two_layers(nc, *args)
    nc.compile()
    r = _run(nc, [arrays], core_ids=[0])
    return r.results[0]["out_0_dram"]
```

```python
import concourse.bass as bass
from concourse import mybir
from contextlib import ExitStack



def gnn_two_layers(nc, x, adj, w_fc, b_fc, w_att, b_att, w1, a1, gamma, beta, out):
    f32 = mybir.dt.float32
    bf16 = mybir.dt.bfloat16
    f16 = mybir.dt.float16
    f8 = mybir.dt.float8e4
    i32 = mybir.dt.int32
    u32 = mybir.dt.uint32
    u16 = mybir.dt.uint16
    i8 = mybir.dt.int8
    u8 = mybir.dt.uint8
    ALU = mybir.AluOpType
    ACT = mybir.ActivationFunctionType
    AX = mybir.AxisListType.X

    N, D = x.shape
    P = 128
    NB = N // P
    NT = NB // 2
    HEADS = 4
    DH = D // HEADS
    C0 = D + 1
    W0 = 3 * C0 + 1
    C1 = DH + 1
    W1 = 3 * C1
    E0, E1 = D + 2, D + 2 * HEADS
    HALF = N // 2
    GB = NB // 2
    EPS = 1e-5
    SLOPE = 0.2
    ONE = 56
    BANK = 512

    x_v = x.rearrange("(t m p) d -> m t (p d)", m=P, p=2)
    out_v = out.rearrange("(t m p) d -> m t (p d)", m=P, p=2)
    adj_v = adj.rearrange("(t m p) j -> t p m j", m=P, p=2)
    x1_dram = nc.dram_tensor("x1_rows", (P, NT, 2 * D), f32, kind="Internal").ap()
    si_dram = nc.dram_tensor("si_rows", (HEADS * NB, P), f32, kind="Internal").ap()

    ctx = ExitStack()
    with ctx:
        def sb(name, shape, dt):
            return ctx.enter_context(nc.sbuf_tensor(name, shape, dt))

        def sem(name):
            return ctx.enter_context(nc.semaphore(name))

        def part(arena, at, shape, dt):
            size = mybir.dt.size(dt)
            n = size
            for k in shape:
                n *= k
            v = arena[:, at:at + n].bitcast(dt)
            if len(shape) == 2:
                v = v.rearrange("p (a b) -> p a b", b=shape[1])
            if len(shape) == 3:
                v = v.rearrange("p (a b c) -> p a b c", b=shape[1], c=shape[2])
            if len(shape) == 4:
                v = v.rearrange("p (a b c d) -> p a b c d", b=shape[1], c=shape[2], d=shape[3])
            return v

        adjT = sb("adjT", [P, NT * N], u16)
        adj_word = adjT[:, :].rearrange("p (t i) -> p t i", i=N)
        adj_u32 = adjT[:, :].bitcast(u32).rearrange("p (t i) -> p t i", i=N // 2)
        adj_f8 = adjT[:, :].bitcast(f8).rearrange("p (t i b) -> p t i b", i=N, b=2)

        hx = sb("hx", [P, NB, E1], f32)

        arena_a = sb("arena_a", [P, 40960], u8)
        stage = [part(arena_a, q * 8192, [HALF], i32) for q in range(4)]
        mask = [part(arena_a, 32768 + q * 2048, [HALF], u8) for q in range(2)]
        words = [part(arena_a, 36864 + q * 2048, [HALF // 2], f16) for q in range(2)]
        srow = [part(arena_a, g * 8192, [HALF], f32) for g in range(2)]
        cmp_i8 = [part(arena_a, 16384 + k * 4096, [HALF, 2], i8) for k in range(2)]
        cmp_u32 = [part(arena_a, 16384 + k * 4096, [HALF // 2], u32) for k in range(2)]
        q_u32 = [[part(arena_a, 24576 + (2 * k + b) * 4096, [HALF // 2], u32) for b in range(2)]
                 for k in range(2)]
        q_f8 = [[part(arena_a, 24576 + (2 * k + b) * 4096, [HALF, 2], f8) for b in range(2)]
                for k in range(2)]

        arena_b = sb("arena_b", [P, NB * W0 * 2], u8)
        v0 = part(arena_b, 0, [NB, W0], bf16)
        v0_parts = v0[:, :, 0:3 * C0].rearrange("p j (c s) -> p j c s", s=3)
        xin = part(arena_b, 0, [NB, D], f32)
        wt = part(arena_b, 16384, [2, D], f32)
        wa0 = part(arena_b, 17408, [2], f32)
        wa1 = part(arena_b, 17416, [2 * HEADS], f32)
        bcol = part(arena_b, 17448, [1], f32)
        raw0 = part(arena_b, 18432, [NB, 6], f32)
        bcol_wide = part(arena_b, 17456, [P], f32)
        v1 = part(arena_b, 0, [NB, 2, W1], bf16)
        v1_bytes = NB * 2 * W1 * 2
        res = [part(arena_b, v1_bytes + g * GB * 2 * C1 * 4, [GB, 2, C1], f32) for g in range(2)]
        tot = part(arena_b, v1_bytes + 2 * GB * 2 * C1 * 4, [GB, C1], f32)
        at_b = v1_bytes + 2 * GB * 2 * C1 * 4 + GB * C1 * 4
        prod_pool = part(arena_b, at_b, [4, 2, C1], f32)

        arena_c = sb("arena_c", [P, GB * C1 * 4], u8)
        xb = part(arena_c, 0, [2, 2, D], f32)
        tmp = part(arena_c, 0, [GB, C1], f32)

        arena_d = sb("arena_d", [P, 2 * E0 * 4], u8)
        wx0 = part(arena_d, 0, [E0], f32)
        bias0 = part(arena_d, E0 * 4, [E0], f32)
        ac = part(arena_d, 0, [HEADS, 2, NB], f32)

        ident = sb("ident", [P, P], f32)
        ident_h = sb("ident_h", [P, P], f16)
        ones = sb("ones", [P, P], f32)
        wx1 = sb("wx1", [P, E1], f32)
        hsum0 = sb("hsum0", [P, D], f32)
        hsum1 = sb("hsum1", [P, HEADS, C1], f32)
        gam = sb("gam", [P, D], f32)
        bet = sb("bet", [P, D], f32)
        agg = sb("agg", [P, 2, C0], f32)
        cent = sb("cent", [P, 2, D], f32)
        hT = sb("hT", [P, 2, D], f32)
        stats = sb("stats", [P, 2, 6], f32)
        mv = sb("mv", [P, NB, 2], f32)
        std = sb("std", [P, NB], f32)
        rstd = sb("rstd", [P, NB], f32)
        bd = sb("bd", [P, HEADS, NB, 2], f32)
        nsj = sb("nsj", [P, HEADS, NB], f32)
        lone = sb("lone", [P, NB], f32)
        fac = sb("fac", [P, NB], f32)
        wj = sb("wj", [P, NB], f32)
        small = sb("small", [P, 16], f32)
        eps = sb("eps", [P, 1], f32)
        max_neg = sb("max_neg", [P, 1], f32)
        max4 = sb("max4", [P, HEADS], f32)
        diag4 = sb("diag4", [HEADS, HEADS], f32)
        batt = sb("batt", [P, 1], f32)
        colsum = bd[:, :, :, :].rearrange("p h j k -> p (h j k)")[:, 0:D]
        t_a = cent[:, 0, :].rearrange("p (h b) -> p h b", b=NB)
        t_b = cent[:, 1, :].rearrange("p (h b) -> p h b", b=NB)
        t_c = hT[:, 0, :].rearrange("p (h b) -> p h b", b=NB)
        siT = hT[:, 1, :]
        den = hT[:, 1, :].rearrange("p (h b) -> p h b", b=NB)
        si_flat = agg[:, :, :].rearrange("p k c -> p (k c)")[:, 0:HEADS * NB]

        ps = ctx.enter_context(nc.psum_tensor("ps", [P, 8 * BANK], f32))
        ps_words = [ps[:, k * BANK:(k + 1) * BANK].bitcast(f16) for k in range(2)]
        ps_l0 = [[ps[:, (2 + 2 * u + k) * BANK:(2 + 2 * u + k) * BANK + W0] for k in range(2)]
                 for u in range(2)]
        ps_l0_pair = [ps[:, (2 + 2 * u) * BANK:(4 + 2 * u) * BANK].rearrange("p (k c) -> p k c", k=2)
                      for u in range(2)]
        ps_t = ps[:, 6 * BANK:6 * BANK + 2 * D].rearrange("p (k c) -> p k c", k=2)
        ps_p = ps[:, 7 * BANK:7 * BANK + 2 * E1].rearrange("p (k c) -> p k c", k=2)
        ps_t2 = [ps_t, ps[:, 4 * BANK:4 * BANK + 2 * D].rearrange("p (k c) -> p k c", k=2)]
        ps_p2 = [ps_p, ps[:, 5 * BANK:5 * BANK + 2 * E1].rearrange("p (k c) -> p k c", k=2)]
        hT2 = [hT[:, :, :], cent[:, :, :]]
        ps_acc = ps[:, :].rearrange("p (b c) -> p b c", c=BANK)

        waits_passed = sem("waits_passed")
        x_in = sem("x_in")
        w_in = sem("w_in")
        wa1_zero = sem("wa1_zero")
        zeros = sem("zeros")
        consts = sem("consts")
        adj_in = [sem(f"adj_in{q}") for q in range(4)]
        xb_in = [sem(f"xb_in{u}") for u in range(2)]
        x1_stored = [sem(f"x1_stored{u}") for u in range(2)]
        stats_made = sem("stats_made")
        aggr_made = sem("aggr_made")
        bcol_made = sem("bcol_made")
        w_T = sem("w_T")
        wt_made = sem("wt_made")
        wx_done = sem("wx_done")
        wx_made = sem("wx_made")
        std0_made = sem("std0_made")
        rstd0_made = sem("rstd0_made")
        h0_made = sem("h0_made")
        hsum_done = sem("hsum_done")
        hsum_read = sem("hsum_read")
        max_part = sem("max_part")
        max_row = sem("max_row")
        max_one = sem("max_one")
        max_all = sem("max_all")
        neg_made = sem("neg_made")
        fac_steps = sem("fac_steps")
        fac_made = sem("fac_made")
        wj_made = sem("wj_made")
        one_made = sem("one_made")
        v0_rest = sem("v0_rest")
        v0_cast = sem("v0_cast")
        masked = sem("masked")
        masked_pool = sem("masked_pool")
        colsum_steps = sem("colsum_steps")
        v0_scaled = sem("v0_scaled")
        packed = sem("packed")
        transposed = sem("transposed")
        adj_kept = sem("adj_kept")
        l0_done = sem("l0_done")
        l0_read = sem("l0_read")
        epi = sem("epi")
        x1_made = sem("x1_made")
        mv_made = sem("mv_made")
        std_made = sem("std_made")
        rstd_made = sem("rstd_made")
        cent_made = sem("cent_made")
        cent_T = sem("cent_T")
        hT_made = sem("hT_made")
        proj_done = sem("proj_done")
        h1_made = sem("h1_made")
        tr_max = sem("tr_max")
        tr_diag = sem("tr_diag")
        tr_pe = sem("tr_pe")
        tr_steps = sem("tr_steps")
        bexp_in = sem("bexp_in")
        aexp_in = sem("aexp_in")
        si_flat_made = sem("si_flat_made")
        si_T = sem("si_T")
        exps_made = sem("exps_made")
        siT_made = sem("siT_made")
        hsum1_done = sem("hsum1_done")
        si_out = sem("si_out")
        srow_in = [sem(f"srow_in{g}") for g in range(2)]
        cmp_act = sem("cmp_act")
        cmp_dve = sem("cmp_dve")
        q_made = sem("q_made")
        rest_made = sem("rest_made")
        pv_done = sem("pv_done")
        bank_done = sem("bank_done")
        bank_read = sem("bank_read")
        v1_made = sem("v1_made")
        v1_chain = sem("v1_chain")
        fin_chain = sem("fin_chain")
        head_out = sem("head_out")
        o_rden = sem("o_rden")
        o_scaled = sem("o_scaled")
        o_stats = sem("o_stats")
        o_aggr = sem("o_aggr")
        o_std = sem("o_std")
        o_rstd = sem("o_rstd")
        o_bias_made = sem("o_bias_made")
        o_x1 = [sem(f"o_x1_{k}") for k in range(2)]
        o_xbeta = sem("o_xbeta")
        o_norm = sem("o_norm")
        o_gam = sem("o_gam")
        o_made = sem("o_made")
        o_out = [sem(f"o_out{k}") for k in range(2)]

        NU = NT
        BANKS = 8
        EPI = 7
        POOL_Q = (0,)
        DVE_Q = tuple(q for q in range(4) if q not in POOL_Q)
        V1_LINKS = 6
        CH = 4
        NCH = NB // CH
        OG = 4
        NOG = NB // OG
        V0_STEPS = [(c, s) for k in range(NCH + 2) for s in range(3) for c in [k - s] if 0 <= c < NCH]
        V0_COUNT = {cs: n + 1 for n, cs in enumerate(V0_STEPS)}
        V0_RESTS = [cs for cs in V0_STEPS if cs[1] > 0]
        V0_REST_COUNT = {cs: n + 1 for n, cs in enumerate(V0_RESTS)}
        o_x1_buf = [part(arena_a, k * 2048, [OG, D], f32) for k in range(2)]
        o_y_buf = [part(arena_a, 4096 + k * 2048, [OG, D], f32) for k in range(2)]
        o_bias = part(arena_a, 8192, [NB], f32)
        o_raw = part(arena_a, 8704, [NB, 6], f32)

        def flat(ap):
            return ap.rearrange("p a c -> p (a c)")

        def row(t3, b, cols=None):
            v = t3[:, bass.ds(b, 1), :] if cols is None else t3[:, bass.ds(b, 1), cols]
            return flat(v)

        def wait_value(eng, signal, value):
            eng.wait_ge(signal, value).then_inc(waits_passed, 1)

        def mean_variance(dve, raw, done):
            even, odd = raw[:, :, 1], raw[:, :, 4]
            total, gap, gap2 = [cent[:, 0, n * NB:(n + 1) * NB] for n in range(3)]
            nc.vector.tensor_tensor(gap, even, odd, ALU.subtract).then_inc(done, 1)
            nc.vector.tensor_tensor(total, even, odd, ALU.add).then_inc(done, 1)
            nc.vector.tensor_tensor(mv[:, :, 1], raw[:, :, 2], raw[:, :, 5], ALU.add).then_inc(done, 1)
            dve.wait_ge(done, 3)
            nc.vector.tensor_scalar(mv[:, :, 0], total, 0.5, None, ALU.mult).then_inc(done, 1)
            nc.vector.tensor_tensor(gap2, gap, gap, ALU.mult).then_inc(done, 1)
            nc.vector.tensor_scalar(mv[:, :, 1], mv[:, :, 1], 1.0 / D, None, ALU.mult).then_inc(done, 1)
            dve.wait_ge(done, 6)
            nc.vector.scalar_tensor_tensor(out=mv[:, :, 1], in0=gap2, scalar=0.25, in1=mv[:, :, 1],
                                           op0=ALU.mult, op1=ALU.add).then_inc(done, 1)

        block = ctx.enter_context(nc.Block())

        @block.sync
        def _(sp):
            sp.dma_start(xin.rearrange("p (t q) d -> p t (q d)", q=2), x_v).then_inc(x_in, 16)

            def masks_read(t, q):
                if q in POOL_Q:
                    sp.wait_ge(masked_pool, t * len(POOL_Q) + POOL_Q.index(q) + 1 - len(POOL_Q))
                else:
                    at = DVE_Q.index(q)
                    sp.wait_ge(masked, t * len(DVE_Q) + at + 1 - len(DVE_Q))

            def body(t, u, has0, has1, has3, half):
                v = 1 - u
                for q in range(4):
                    if has0:
                        if not isinstance(t, int) or t > 0:
                            masks_read(t, q)
                        sp.dma_start(stage[q], adj_v[t, q // 2][:, (q % 2) * HALF:(q % 2 + 1) * HALF])\
                          .then_inc(adj_in[q], 16)
                    if q == 1 and has3:
                        sp.wait_ge(x1_made, t - 2)
                        sp.dma_start(x1_dram[:, t - 3], flat(xb[:, v])).then_inc(x1_stored[v], 16)
                if has1:
                    if has3:
                        wait_value(sp, x1_stored[v], (half if u else half - 1) * 16)
                        sp.wait_ge(cent_made, t + NT - 2)
                    sp.dma_start(flat(xb[:, v]), x_v[:, t - 1]).then_inc(xb_in[v], 16)

            body(0, 0, True, False, False, 0)
            body(1, 1, True, True, False, 0)
            body(2, 0, True, True, False, 1)
            body(3, 1, True, True, True, 1)
            with sp.Fori(2, NT // 2) as half:
                body(half * 2, 0, True, True, True, half)
                body(half * 2 + 1, 1, True, True, True, half)
            body(NT, 0, False, True, True, NT // 2)
            body(NT + 1, 1, False, False, True, NT // 2)
            body(NT + 2, 0, False, False, True, NT // 2 + 1)

            sp.wait_ge(siT_made, 1)
            sp.dma_start(si_dram, siT).then_inc(si_out, 16)
            sp.wait_ge(si_out, 16)
            si_v = si_dram.rearrange("(h g b) m -> h g (b m)", h=HEADS, g=2)

            def rows(h, g):
                sp.dma_start(srow[g], si_v[h, g].partition_broadcast(P)).then_inc(srow_in[g], 16)

            rows(0, 0)
            rows(0, 1)
            with sp.Fori(1, HEADS) as h:
                for g in range(2):
                    wait_value(sp, cmp_act, h * (2 * NU) + (g + 1 - 2) * NU)
                    wait_value(sp, q_made, h * (2 * NU) + (g + 1 - 2) * NU + 2)
                    rows(h, g)

            def x1_load(n, k):
                sp.dma_start(o_x1_buf[k].rearrange("p (t q) d -> p t (q d)", q=2),
                             x1_dram[:, n * (OG // 2):(n + 1) * (OG // 2)]).then_inc(o_x1[k], 16)

            for u in range(2):
                sp.wait_ge(x1_stored[u], 16 * (NT // 2))
            sp.wait_ge(head_out, 2 * HEADS + 2)
            x1_load(0, 0)
            x1_load(1, 1)
            for n in range(NOG):
                k = n % 2
                sp.wait_ge(o_made, n + 1)
                sp.dma_start(out_v[:, n * (OG // 2):(n + 1) * (OG // 2)],
                             o_y_buf[k].rearrange("p (t q) d -> p t (q d)", q=2)).then_inc(o_out[k], 16)
                if n + 2 < NOG:
                    x1_load(n + 2, k)
            for k in range(2):
                sp.wait_ge(o_out[k], 16 * (NOG // 2))

        @block.gpsimd
        def _(pool):
            nc.gpsimd.memset(wa1, 0.0).then_inc(wa1_zero, 1)
            nc.gpsimd.memset(ident[:, :], 0.0).then_inc(zeros, 1)
            nc.gpsimd.memset(ident_h[:, :], 0.0).then_inc(zeros, 1)
            nc.gpsimd.memset(ones[:, :], 1.0).then_inc(consts, 1)
            nc.gpsimd.memset(eps[:, :], EPS).then_inc(consts, 1)
            nc.gpsimd.memset(hsum1[:, :, DH:C1], float(N)).then_inc(head_out, 2)
            pool.wait_ge(zeros, 2)
            for m in (ident, ident_h):
                nc.gpsimd.affine_select(out=m[:, :], in_=m[:, :], compare_op=ALU.not_equal, fill=1.0,
                                        base=0, pattern=[[-1, P]], channel_multiplier=1).then_inc(consts, 1)

            def add_to_colsum(B, k):
                nc.gpsimd.tensor_tensor(colsum[:, :], colsum[:, :], row(hx, B, slice(0, D)), ALU.add)\
                    .then_inc(colsum_steps, 1)
                wait_value(pool, colsum_steps, k)

            def compare(t):
                for n, q in enumerate(POOL_Q):
                    if not isinstance(t, int) or 4 * t + q >= 2:
                        wait_value(pool, packed, t * 4 + q - 1)
                    wait_value(pool, adj_in[q], t * 16 + 16)
                    nc.gpsimd.tensor_scalar(mask[q % 2], stage[q], 1.0, 0.0, ALU.min, ALU.max)\
                        .then_inc(masked_pool, 1)

            compare(0)
            nc.gpsimd.memset(colsum[:, :], 0.0).then_inc(colsum_steps, 1)
            pool.wait_ge(colsum_steps, 1)
            for t in range(NT):
                pool.wait_ge(h0_made, t + 1)
                for k in range(2):
                    add_to_colsum(2 * t + k, 2 * t + k + 2)
            pool.wait_ge(one_made, 2)
            pool.wait_ge(wj_made, 1)
            for c in range(NCH):
                js = slice(c * CH, (c + 1) * CH)
                nc.gpsimd.tensor_tensor(hx[:, js, 0:C0], hx[:, js, 0:C0],
                                        wj[:, js].unsqueeze(2).to_broadcast([P, CH, C0]), ALU.mult)\
                    .then_inc(v0_scaled, 1)
            pool.wait_ge(hsum_done, 1)
            nc.gpsimd.memset(colsum[:, :], 0.0).then_inc(colsum_steps, 1)
            pool.wait_ge(colsum_steps, NB + 2)

            def sums(s):
                wait_value(pool, h1_made, s * 2 + 2)
                for k in range(2):
                    add_to_colsum(s * 2 + k, s * 2 + (k + NB + 3))

            for t in range(1, 4):
                compare(t)
            with pool.Fori(4, NT) as t:
                compare(t)
                sums(t - 4)
            for t in range(NT, NT + 4):
                sums(t - 4)

            def build(h, c):
                js = slice(c * CH, (c + 1) * CH)
                dst = v1[:, js].rearrange("p j b (c s) -> p (j b) c s", s=3)
                prod = prod_pool.rearrange("p j b c -> p (j b) c")
                base = h * (NCH * V1_LINKS) + c * V1_LINKS

                def link(ins, k):
                    ins.then_inc(v1_chain, 1)
                    wait_value(pool, v1_chain, base + k)

                if not isinstance(h, int) or c > 0:
                    wait_value(pool, v1_made, h * NCH + c)
                bd_h = bd[:, bass.ds(h, 1), js, :].rearrange("p a j b -> p (a j) b")
                nc.gpsimd.tensor_copy(prod_pool[:, :, :, DH], bd_h)
                for b in range(2):
                    last = nc.gpsimd.tensor_tensor(prod_pool[:, :, b, 0:DH], hx[:, js, bass.ds(h * DH, DH)],
                                                   bd_h[:, :, b].unsqueeze(2).to_broadcast([P, CH, DH]),
                                                   ALU.mult)
                    link(last, b + 1)
                link(nc.gpsimd.tensor_copy(dst[:, :, :, 0], prod), 3)
                link(nc.gpsimd.tensor_tensor(prod, prod, dst[:, :, :, 0], ALU.subtract), 4)
                link(nc.gpsimd.tensor_copy(dst[:, :, :, 1], prod), 5)
                link(nc.gpsimd.tensor_tensor(prod, prod, dst[:, :, :, 1], ALU.subtract), 6)
                nc.gpsimd.tensor_copy(dst[:, :, :, 2], prod).then_inc(v1_made, 1)

            FIN = 4

            def finish(h, g):
                blk = slice(g * GB, (g + 1) * GB)

                def link(ins, k):
                    ins.then_inc(fin_chain, 1)
                    wait_value(pool, fin_chain, (h * 2 + g) * FIN + k)

                def factor(k):
                    return ac[:, bass.ds(h, 1), k, blk].rearrange("p a b -> p (a b)").unsqueeze(2)\
                        .to_broadcast([P, GB, C1])

                wait_value(pool, bank_read, (h * 2 + g + 2) * BANKS)
                wait_value(pool, head_out, h * 2 + g + 2)
                nc.gpsimd.tensor_tensor(tot, res[g][:, :, 0, :], factor(0), ALU.mult)
                link(nc.gpsimd.tensor_tensor(tmp, res[g][:, :, 1, :], factor(1), ALU.mult), 1)
                link(nc.gpsimd.tensor_tensor(tot, tot, tmp, ALU.add), 2)
                link(nc.gpsimd.tensor_tensor(tmp, lone[:, blk].unsqueeze(2).to_broadcast([P, GB, C1]),
                                             hsum1[:, bass.ds(h, 1), :].to_broadcast([P, GB, C1]),
                                             ALU.mult), 3)
                link(nc.gpsimd.tensor_tensor(tot, tot, tmp, ALU.add), 4)
                nc.gpsimd.tensor_copy(den[:, bass.ds(h, 1), blk].rearrange("p a b -> p (a b)"), tot[:, :, DH])
                nc.gpsimd.tensor_copy(hx[:, blk, bass.ds(h * DH, DH)], tot[:, :, 0:DH]).then_inc(head_out, 1)

            pool.wait_ge(exps_made, 4)
            for c in range(NCH):
                build(0, c)
            pool.wait_ge(head_out, 2)
            with pool.Fori(0, HEADS - 1) as h:
                finish(h, 0)
                for c in range(NCH):
                    wait_value(pool, pv_done, h * (2 * NU) + NU + (c + 1) * (CH // 2) + 2)
                    build(h + 1, c)
                finish(h, 1)
            finish(HEADS - 1, 0)
            finish(HEADS - 1, 1)

            for n in range(NOG):
                k = n % 2
                pool.wait_ge(o_x1[k], 16 * (n // 2 + 1))
                nc.gpsimd.tensor_tensor(o_x1_buf[k], o_x1_buf[k],
                                        bet[:, :].unsqueeze(1).to_broadcast([P, OG, D]), ALU.add)\
                    .then_inc(o_xbeta, 1)

        @block.scalar
        def _(act):
            act.dma_start(wx0[:, 0:D], w_fc).then_inc(w_in, 16)
            act.dma_start(wx1[:, 0:D], w1).then_inc(w_in, 16)
            for k in range(2):
                act.dma_start(wa0[:, k:k + 1], w_att[k * D:(k + 1) * D].rearrange("(n a) -> n a", a=1))\
                   .then_inc(w_in, 16)
            act.dma_start(bcol, b_fc.rearrange("(n a) -> n a", a=1)).then_inc(w_in, 16)
            act.dma_start(batt[:, :], b_att.partition_broadcast(P)).then_inc(w_in, 16)
            act.dma_start(gam[:, :], gamma.partition_broadcast(P)).then_inc(w_in, 16)
            act.dma_start(bet[:, :], beta.partition_broadcast(P)).then_inc(w_in, 16)
            act.wait_ge(wa1_zero, 1)
            for h in range(HEADS):
                for k in range(2):
                    act.dma_start(wa1[h * DH:(h + 1) * DH, k * HEADS + h:k * HEADS + h + 1],
                                  a1[k * DH:(k + 1) * DH, :]).then_inc(w_in, 16)

            act.wait_ge(aggr_made, 7)
            act.wait_ge(consts, 4)
            nc.scalar.activation(std[:, :], mv[:, :, 1], ACT.Sqrt, bias=eps[:, :]).then_inc(std0_made, 1)
            def copy_turned(t, u, free):
                act.wait_ge(cent_T, t + 1)
                if free:
                    act.wait_ge(proj_done, t - 1)
                nc.scalar.activation(hT2[u], ps_t2[u], ACT.Copy).then_inc(hT_made, 1)

            copy_turned(0, 0, False)
            copy_turned(1, 1, False)
            with act.Fori(1, NT // 2) as tt:
                copy_turned(tt * 2, 0, True)
                copy_turned(tt * 2 + 1, 1, True)
            act.wait_ge(neg_made, 1)
            nc.scalar.activation(wj[:, :], hx[:, :, D + 1], ACT.Exp, bias=max_neg[:, :]).then_inc(wj_made, 1)
            act.wait_ge(fac_made, 1)
            nc.scalar.activation(fac[:, :], fac[:, :], ACT.Exp).then_inc(wj_made, 1)
            for c, s in V0_STEPS:
                js = slice(c * CH, (c + 1) * CH)
                if s == 0:
                    act.wait_ge(v0_scaled, c + 1)
                else:
                    act.wait_ge(v0_rest, V0_REST_COUNT[c, s])
                nc.scalar.activation(v0_parts[:, js, :, s], hx[:, js, 0:C0], ACT.Copy).then_inc(v0_cast, 1)

            def body(t, u, has0, has3):
                def keep(q):
                    act.wait_ge(transposed, t * 4 + q + 1)
                    nc.scalar.activation(
                        adj_word[:, (q % 2) * (NT // 2):(q % 2 + 1) * (NT // 2),
                                 bass.ds(t * (2 * P) + (q // 2) * P, P)],
                        ps_words[q % 2].rearrange("p (a m) -> p a m", m=P), ACT.Copy,
                        scale=float(ONE)).then_inc(adj_kept, 1)
                v = 1 - u
                if has3:
                    act.wait_ge(mv_made, t - 2)
                    nc.scalar.activation(std[:, 0:2], mv[:, 0:2, 1], ACT.Sqrt, bias=eps[:, :])\
                        .then_inc(std_made, 1)
                if has0:
                    keep(0)
                    keep(1)
                if has3:
                    act.wait_ge(cent_T, t + (NT - 2))
                    nc.scalar.activation(hT[:, :, :], ps_t, ACT.Copy).then_inc(hT_made, 1)
                if has0:
                    keep(2)
                    keep(3)
                if has3:
                    act.wait_ge(proj_done, t + (NT - 2))
                    act.wait_ge(rstd_made, t - 2)
                    for k in range(2):
                        nc.scalar.activation(row(hx, t * 2 + (k - 6)), ps_p[:, k, :], ACT.Copy,
                                             scale=rstd[:, 2 * v + k:2 * v + k + 1]).then_inc(h1_made, 1)

            body(0, 0, True, False)
            body(1, 1, True, False)
            body(2, 0, True, False)
            body(3, 1, True, True)
            with act.Fori(2, NT // 2) as half:
                body(half * 2, 0, True, True)
                body(half * 2 + 1, 1, True, True)
            for t in range(NT, NT + 3):
                body(t, t % 2, False, True)

            act.wait_ge(bexp_in, 1)
            act.wait_ge(hsum1_done, 1)
            for k, slope in enumerate((1.0, SLOPE)):
                nc.scalar.activation(bd[:, :, :, k], t_a, ACT.Exp, scale=slope).then_inc(exps_made, 1)
            act.wait_ge(aexp_in, 2)
            for k, t_k in enumerate((t_b, t_c)):
                nc.scalar.activation(ac[:, :, k, :], t_k, ACT.Exp).then_inc(exps_made, 1)
            act.wait_ge(si_T, 1)
            nc.scalar.activation(siT, ps[:, 2 * BANK:2 * BANK + P], ACT.Copy).then_inc(siT_made, 1)

            with act.Fori(0, HEADS) as h:
                for g in range(2):
                    wait_value(act, srow_in[g], h * 16 + 16)
                    with act.Fori(0, NU // 2) as jj:
                        for k in range(2):
                            act.wait_ge(q_made, h * (2 * NU) + g * NU + jj * 2 + k + 1)
                            for p in range(k + 1):
                                last = nc.scalar.activation(
                                    cmp_i8[k][:, :, p], srow[g], ACT.Sign, scale=-1.0,
                                    bias=row(nsj, h, bass.ds(jj * 4 + 2 * k + p, 1)))
                            last.then_inc(cmp_act, 1)

            act.wait_ge(o_aggr, 7)
            nc.scalar.activation(std[:, :], mv[:, :, 1], ACT.Sqrt, bias=eps[:, :]).then_inc(o_std, 1)
            act.wait_ge(o_bias_made, 1)
            for n in range(NOG):
                k = n % 2
                if n >= 2:
                    act.wait_ge(o_out[k], 16 * (n // 2))
                for b in range(OG):
                    B = n * OG + b
                    last = nc.scalar.activation(o_y_buf[k][:, b, :], hx[:, B, 0:D], ACT.Identity,
                                                scale=rstd[:, B:B + 1], bias=o_bias[:, B:B + 1])
                last.then_inc(o_norm, 1)

        @block.vector
        def _(dve):
            dve.wait_ge(x_in, 16)
            for b in range(NB):
                nc.vector.bn_stats(raw0[:, b, :], xin[:, b, :]).then_inc(stats_made, 1)
            dve.wait_ge(stats_made, NB)
            mean_variance(dve, raw0, aggr_made)
            dve.wait_ge(w_in, 16 * (8 + 2 * HEADS))
            dve.wait_ge(consts, 4)
            nc.vector.tensor_scalar(bcol_wide, ones[:, :], bcol, None, ALU.mult).then_inc(bcol_made, 1)
            dve.wait_ge(w_T, 1)
            nc.vector.tensor_copy(wt, ps_t).then_inc(wt_made, 1)
            dve.wait_ge(wx_done, 1)
            at = 7 * BANK
            nc.vector.tensor_copy(wx0[:, D:E0], ps[:, at:at + 2])
            nc.vector.tensor_copy(wx1[:, D:E1], ps[:, at + 2:at + 2 + 2 * HEADS])
            nc.vector.tensor_copy(bias0[:, :], ps[:, at + 16:at + 16 + E0]).then_inc(wx_made, 1)
            dve.wait_ge(std0_made, 1)
            nc.vector.reciprocal(rstd[:, :], std[:, :]).then_inc(rstd0_made, 1)
            dve.wait_ge(rstd0_made, 1)
            dve.wait_ge(wx_made, 1)

            def center(t):
                for k in range(2):
                    last = nc.vector.tensor_scalar(row(xin, t * 2 + k), row(xin, t * 2 + k),
                                                   row(mv, t * 2 + k, slice(0, 1)), 0.0,
                                                   ALU.subtract, ALU.max)
                last.then_inc(cent_made, 1)

            def scaled(t, u):
                dve.wait_ge(proj_done, t + 1)
                for k in range(2):
                    last = nc.vector.scalar_tensor_tensor(
                        out=row(hx, t * 2 + k, slice(0, E0)), in0=ps_p2[u][:, k, 0:E0],
                        scalar=rstd[:, bass.ds(t * 2 + k, 1)], in1=bias0[:, :], op0=ALU.mult, op1=ALU.add)
                last.then_inc(h0_made, 1)

            for t in range(4):
                center(t)
            with dve.Fori(2, NT // 2) as tt:
                for u in range(2):
                    center(tt * 2 + u)
                    scaled(tt * 2 + (u - 4), u)
            for t in range(NT - 4, NT):
                scaled(t, t % 2)
            dve.wait_ge(h0_made, NT)

            nc.vector.reduce_max(small[:, 0:1], hx[:, :, D + 1], AX).then_inc(max_part, 1)
            nc.vector.tensor_scalar(fac[:, :], hx[:, :, D], batt[:, :], None, ALU.add).then_inc(fac_steps, 1)
            dve.wait_ge(max_row, 1)
            nc.vector.reduce_max(small[0:1, 2:3], ps[0:1, 6 * BANK:6 * BANK + P], AX).then_inc(max_one, 1)
            dve.wait_ge(max_all, 1)
            nc.vector.tensor_scalar(max_neg[:, :], ps[:, 7 * BANK:7 * BANK + 1], -1.0, None, ALU.mult)\
                .then_inc(neg_made, 1)
            dve.wait_ge(neg_made, 1)
            dve.wait_ge(fac_steps, 1)
            nc.vector.tensor_scalar(std[:, :], fac[:, :], max_neg[:, :], None, ALU.subtract)\
                .then_inc(fac_steps, 1)
            dve.wait_ge(fac_steps, 2)
            nc.vector.scalar_tensor_tensor(out=fac[:, :], in0=fac[:, :], scalar=max_neg[:, :],
                                           in1=std[:, :], op0=ALU.subtract, op1=ALU.subtract)\
                .then_inc(fac_made, 1)
            nc.vector.memset(hx[:, :, D:C0], 1.0).then_inc(one_made, 1)
            nc.vector.memset(v0[:, :, W0 - 1:W0], 1.0).then_inc(one_made, 1)
            dve.wait_ge(hsum_done, 1)
            nc.vector.tensor_copy(hsum0[:, :], ps[:, 3 * BANK:3 * BANK + D]).then_inc(hsum_read, 1)
            for c, s in V0_RESTS:
                js = slice(c * CH, (c + 1) * CH)
                dve.wait_ge(v0_cast, V0_COUNT[c, s - 1])
                nc.vector.tensor_tensor(hx[:, js, 0:C0], hx[:, js, 0:C0], v0_parts[:, js, :, s - 1],
                                        ALU.subtract).then_inc(v0_rest, 1)
            dve.wait_ge(wj_made, 2)

            def take(t, u, has0, has2, has3, half):
                s, v = t - 2, 1 - u

                def compare(q):
                    if not has0:
                        return
                    if not isinstance(t, int) or 4 * t + q >= 2:
                        dve.wait_ge(packed, t * 4 + q - 1)
                    dve.wait_ge(adj_in[q], t * 16 + 16)
                    nc.vector.tensor_scalar(mask[q % 2], stage[q], 0.0, None, ALU.is_gt).then_inc(masked, 1)

                def pack(q):
                    if not has0:
                        return
                    if q in POOL_Q:
                        dve.wait_ge(masked_pool, t * len(POOL_Q) + POOL_Q.index(q) + 1)
                    else:
                        dve.wait_ge(masked, t * len(DVE_Q) + DVE_Q.index(q) + 1)
                    if not isinstance(t, int) or 4 * t + q >= 2:
                        dve.wait_ge(transposed, t * 4 + q - 1)
                    pair = mask[q % 2].rearrange("p (w b) -> p w b", b=2)
                    nc.vector.scalar_tensor_tensor(out=words[q % 2], in0=pair[:, :, 1], scalar=256.0,
                                                   in1=pair[:, :, 0], op0=ALU.mult, op1=ALU.add)\
                        .then_inc(packed, 1)

                two = bass.ds(t * 2 - 4, 2)

                def made(k):
                    dve.wait_ge(epi, t * EPI + (k - 2 * EPI))

                def step_sum():
                    dve.wait_ge(l0_done, t * 2 - 2)
                    nc.vector.tensor_reduce(
                        agg[:, :, :], ps_l0_pair[u][:, :, 0:3 * C0].rearrange("p k (c s) -> p k c s", s=3),
                        AX, ALU.add).then_inc(epi, 1)
                    nc.vector.tensor_scalar(lone[:, two], ps_l0_pair[u][:, :, W0 - 1], 0.0, None, ALU.is_equal)\
                        .then_inc(l0_read, 1)

                def step_weight():
                    made(1)
                    nc.vector.tensor_tensor(small[:, 0:2], agg[:, :, D], fac[:, two], ALU.mult).then_inc(epi, 1)

                def step_count():
                    made(2)
                    dve.wait_ge(l0_read, t - 1)
                    nc.vector.scalar_tensor_tensor(out=small[:, 2:4], in0=lone[:, two], scalar=float(N),
                                                   in1=small[:, 0:2], op0=ALU.mult, op1=ALU.add)\
                        .then_inc(epi, 1)

                def step_reciprocal():
                    made(3)
                    nc.vector.reciprocal(small[:, 4:6], small[:, 2:4]).then_inc(epi, 1)

                def step_factors():
                    made(4)
                    nc.vector.tensor_tensor(small[:, 6:8], fac[:, two], small[:, 4:6], ALU.mult)
                    nc.vector.tensor_tensor(small[:, 8:10], lone[:, two], small[:, 4:6], ALU.mult)\
                        .then_inc(epi, 1)

                def step_rows():
                    made(5)
                    dve.wait_ge(xb_in[u], half * 16)
                    for k in range(2):
                        last = nc.vector.scalar_tensor_tensor(
                            out=xb[:, u, k, :], in0=agg[:, k, 0:D], scalar=small[:, 6 + k:7 + k],
                            in1=xb[:, u, k, :], op0=ALU.mult, op1=ALU.add)
                    last.then_inc(epi, 1)

                def step_lone_rows():
                    made(6)
                    for k in range(2):
                        last = nc.vector.scalar_tensor_tensor(
                            out=xb[:, u, k, :], in0=hsum0[:, :], scalar=small[:, 8 + k:9 + k],
                            in1=xb[:, u, k, :], op0=ALU.mult, op1=ALU.add)
                    last.then_inc(x1_made, 1)

                def step_statistics():
                    dve.wait_ge(x1_made, t - 1)
                    for k in range(2):
                        last = nc.vector.bn_stats(stats[:, k, :], xb[:, u, k, :])
                    last.then_inc(epi, 1)
                    wait_value(dve, epi, t * EPI + (7 - 2 * EPI))
                    for k in range(2):
                        last = nc.vector.bn_aggr(mv[:, k, :], stats[:, k, :])
                    last.then_inc(mv_made, 1)

                def center_rstd():
                    dve.wait_ge(std_made, t - 2)
                    if not isinstance(t, int) or t > 3:
                        dve.wait_ge(hT_made, t + (NT - 3))
                    nc.vector.reciprocal(rstd[:, 2 * v:2 * v + 2], std[:, 0:2]).then_inc(rstd_made, 1)

                def center_rows():
                    dve.wait_ge(mv_made, t - 2)
                    if not isinstance(t, int) or t > 3:
                        dve.wait_ge(cent_T, t + (NT - 3))
                    for k in range(2):
                        last = nc.vector.tensor_scalar(cent[:, k, :], xb[:, v, k, :], mv[:, k, 0:1], 0.0,
                                                       ALU.subtract, ALU.max)
                    last.then_inc(cent_made, 1)

                for q in (0, 1):
                    if q in DVE_Q:
                        compare(q)
                if has3:
                    center_rows()
                    center_rstd()
                pack(0)
                if has2:
                    step_sum()
                pack(1)
                if has2:
                    step_weight()
                    if 2 not in DVE_Q:
                        step_count()
                if 2 in DVE_Q:
                    compare(2)
                    if has2:
                        step_count()
                compare(3)
                if has2:
                    step_reciprocal()
                    step_factors()
                pack(2)
                if has2:
                    step_rows()
                pack(3)
                if has2:
                    step_lone_rows()
                    step_statistics()

            take(0, 0, True, False, False, 0)
            take(1, 1, True, False, False, 0)
            take(2, 0, True, True, False, 1)
            take(3, 1, True, True, True, 1)
            with dve.Fori(2, NT // 2) as half:
                take(half * 2, 0, True, True, True, half)
                take(half * 2 + 1, 1, True, True, True, half)
            take(NT, 0, False, True, True, NT // 2)
            take(NT + 1, 1, False, True, True, NT // 2)
            take(NT + 2, 0, False, False, True, NT // 2 + 1)

            dve.wait_ge(h1_made, 2 * NT)
            si = hx[:, :, D:D + HEADS].rearrange("p j h -> p h j")
            sj = hx[:, :, D + HEADS:E1].rearrange("p j h -> p h j")
            nc.vector.reduce_max(max4[:, :], sj, AX).then_inc(tr_max, 1)
            nc.vector.tensor_copy(si_flat.rearrange("p (h j) -> p h j", j=NB), si).then_inc(si_flat_made, 1)
            nc.vector.tensor_scalar(nsj[:, :, :], sj, -1.0, None, ALU.mult).then_inc(q_made, 2)
            dve.wait_ge(q_made, 2)
            dve.wait_ge(tr_pe, 1)
            nc.vector.reduce_max(small[0:HEADS, 0:1], ps[0:HEADS, 6 * BANK:6 * BANK + P], AX)\
                .then_inc(tr_steps, 1)
            dve.wait_ge(tr_steps, 1)
            nc.vector.tensor_scalar(diag4[:, :], ident[0:HEADS, 0:HEADS], small[0:HEADS, 0:1], None, ALU.mult)\
                .then_inc(tr_diag, 1)
            dve.wait_ge(tr_pe, 2)
            nc.vector.tensor_copy(max4[:, :], ps[:, 7 * BANK:7 * BANK + HEADS]).then_inc(tr_steps, 1)
            dve.wait_ge(tr_steps, 2)
            wide = max4[:, :].unsqueeze(2).to_broadcast([P, HEADS, NB])
            nc.vector.tensor_tensor(t_a, sj, wide, ALU.subtract).then_inc(bexp_in, 1)
            nc.vector.tensor_tensor(t_b, si, wide, ALU.add).then_inc(tr_steps, 1)
            dve.wait_ge(tr_steps, 3)
            row_max = xb[:, 0].rearrange("p k d -> p (k d)")[:, 0:HEADS * NB].rearrange("p (h j) -> p h j", j=NB)
            dve.wait_ge(x1_stored[0], 16 * (NT // 2))
            nc.vector.scalar_tensor_tensor(out=row_max, in0=t_b, scalar=SLOPE, in1=t_b, op0=ALU.mult,
                                           op1=ALU.max).then_inc(tr_steps, 1)
            dve.wait_ge(tr_steps, 4)
            nc.vector.scalar_tensor_tensor(out=t_c, in0=t_b, scalar=SLOPE, in1=row_max, op0=ALU.mult,
                                           op1=ALU.subtract).then_inc(aexp_in, 1)
            dve.wait_ge(aexp_in, 1)
            nc.vector.tensor_tensor(t_b, t_b, row_max, ALU.subtract).then_inc(aexp_in, 1)
            dve.wait_ge(hsum1_done, 1)
            nc.vector.tensor_copy(hsum1[:, :, 0:DH], ps[:, 5 * BANK:5 * BANK + D]
                                  .rearrange("p (h d) -> p h d", d=DH)).then_inc(bank_read, BANKS)

            with dve.Fori(0, HEADS) as h:
                for g in range(2):
                    wait_value(dve, srow_in[g], h * 16 + 16)
                    with dve.Fori(0, NU // 2) as jj:
                        for k in range(2):
                            done = h * (2 * NU) + g * NU + jj * 2 + k
                            if k == 0:
                                nc.vector.tensor_scalar(cmp_i8[k][:, :, 1], srow[g],
                                                        row(nsj, h, bass.ds(jj * 4 + 1, 1)), float(ONE),
                                                        ALU.is_gt, ALU.mult).then_inc(cmp_dve, 1)
                                dve.wait_ge(cmp_dve, h * NU + g * (NU // 2) + jj + 1)
                            dve.wait_ge(cmp_act, done + 1)
                            dve.wait_ge(pv_done, done + 1)
                            adj_u = adj_u32[:, bass.ds(jj * 2 + k, 1), g * (HALF // 2):(g + 1) * (HALF // 2)]
                            adj_u = flat(adj_u)
                            nc.vector.tensor_tensor(q_u32[k][0], cmp_u32[k], adj_u, ALU.bitwise_and)\
                                .then_inc(q_made, 1)
                            dve.wait_ge(q_made, done + 3)
                            nc.vector.tensor_tensor(q_u32[k][1], q_u32[k][0], adj_u, ALU.bitwise_xor)\
                                .then_inc(rest_made, 1)
                    dve.wait_ge(head_out, h * 2 + g + 1)
                    for n in range(BANKS):
                        if n < BANKS - 1:
                            dve.wait_ge(bank_done, h * (2 * BANKS - 2) + g * (BANKS - 1) + n + 1)
                        else:
                            dve.wait_ge(pv_done, h * (2 * NU) + (g + 1) * NU + 2)
                        nc.vector.tensor_reduce(
                            res[g][:, 2 * n:2 * n + 2].rearrange("p a b c -> p (a b c)"),
                            ps_acc[:, n, 0:4 * W1].rearrange("p (c s) -> p c s", s=3), AX, ALU.add)\
                            .then_inc(bank_read, 1)

            dve.wait_ge(head_out, 2 * HEADS + 2)
            nc.vector.reciprocal(den, den).then_inc(o_rden, 1)
            dve.wait_ge(o_rden, 1)
            for h in range(HEADS):
                cols = hx[:, :, h * DH:(h + 1) * DH]
                last = nc.vector.tensor_tensor(cols, cols, den[:, h, :].unsqueeze(2)
                                               .to_broadcast([P, NB, DH]), ALU.mult)
            last.then_inc(o_scaled, 1)
            dve.wait_ge(o_scaled, 1)
            for b in range(NB):
                nc.vector.bn_stats(o_raw[:, b, :], hx[:, b, 0:D]).then_inc(o_stats, 1)
            dve.wait_ge(o_stats, NB)
            mean_variance(dve, o_raw, o_aggr)
            dve.wait_ge(o_std, 1)
            nc.vector.reciprocal(rstd[:, :], std[:, :]).then_inc(o_rstd, 1)
            dve.wait_ge(o_rstd, 1)
            nc.vector.scalar_tensor_tensor(out=o_bias, in0=mv[:, :, 0], scalar=-1.0, in1=rstd[:, :],
                                           op0=ALU.mult, op1=ALU.mult).then_inc(o_bias_made, 1)
            for n in range(NOG):
                k = n % 2
                dve.wait_ge(o_norm, n + 1)
                nc.vector.tensor_tensor(o_y_buf[k], o_y_buf[k],
                                        gam[:, :].unsqueeze(1).to_broadcast([P, OG, D]), ALU.mult)\
                    .then_inc(o_gam, 1)
                dve.wait_ge(o_gam, n + 1)
                dve.wait_ge(o_xbeta, n + 1)
                nc.vector.tensor_tensor(o_y_buf[k], o_y_buf[k], o_x1_buf[k], ALU.add).then_inc(o_made, 1)

        @block.tensor
        def _(pe):
            pe.wait_ge(w_in, 16 * (8 + 2 * HEADS))
            pe.wait_ge(consts, 4)
            for k, w in enumerate((wx0, wx1)):
                last = nc.tensor.transpose(ps_t[:, k, :], w[:, 0:D], ident[:, :])
            last.then_inc(w_T, 1)
            pe.wait_ge(wt_made, 1)
            pe.wait_ge(bcol_made, 1)
            at = 7 * BANK
            for o, n, lhsT, rhs in ((0, 2, wt[:, 0, :], wa0), (2, 2 * HEADS, wt[:, 1, :], wa1),
                                    (16, D, bcol_wide, ident[:, :]), (16 + D, 2, bcol_wide, wa0)):
                last = nc.tensor.matmul(ps[:, at + o:at + o + n], lhsT, rhs, start=True, stop=True)
            last.then_inc(wx_done, 1)

            def flip(t, u, rows_of, read):
                pe.wait_ge(cent_made, t + 1)
                if read > 0:
                    pe.wait_ge(hT_made, read)
                for k in range(2):
                    last = nc.tensor.transpose(ps_t2[u][:, k, :], rows_of(k), ident[:, :])
                last.then_inc(cent_T, 1)

            def project(t, u, w, cols):
                pe.wait_ge(hT_made, t + 1)
                for k in range(2):
                    last = nc.tensor.matmul(ps_p2[u][:, k, 0:cols], hT2[u][:, k, :], w[:, 0:cols],
                                            start=True, stop=True)
                last.then_inc(proj_done, 1)

            def column_sums(bank, done):
                nc.tensor.matmul(ps[:, bank * BANK:bank * BANK + D], ones[:, :], colsum[:, :],
                                 start=True, stop=True).then_inc(done, 1)

            pe.wait_ge(wx_made, 1)
            for t in range(NT + 1):
                if t < NT:
                    flip(t, t % 2, lambda k: xin[:, 2 * t + k, :], t - 1)
                if t > 0:
                    if t > 2:
                        pe.wait_ge(h0_made, t - 2)
                    project(t - 1, (t - 1) % 2, wx0, E0)
            pe.wait_ge(max_part, 1)
            nc.tensor.matmul(ps[0:1, 6 * BANK:6 * BANK + P], small[:, 0:1], ident[:, :],
                             start=True, stop=True).then_inc(max_row, 1)
            pe.wait_ge(max_one, 1)
            nc.tensor.matmul(ps[:, 7 * BANK:7 * BANK + 1], ones[0:1, :], small[0:1, 2:3],
                             start=True, stop=True).then_inc(max_all, 1)
            pe.wait_ge(colsum_steps, NB + 1)
            column_sums(3, hsum_done)

            def turn(B):
                for hf in range(2):
                    n = 2 * B + hf
                    pe.wait_ge(packed, n + 1)
                    if n >= 2:
                        pe.wait_ge(adj_kept, n - 1)
                    for a in range(NT // 2):
                        last = nc.tensor.transpose(ps_words[hf][:, a * P:(a + 1) * P],
                                                   words[hf][:, a * P:(a + 1) * P], ident_h[:, :])
                    last.then_inc(transposed, 1)

            def aggregate(B):
                s = B // 2
                pe.wait_ge(adj_kept, 2 * B + 2)
                if B % 2 == 0 and s >= 2:
                    pe.wait_ge(l0_read, s - 1)
                for J in range(NB):
                    if B == 0 and J % CH == 0:
                        pe.wait_ge(v0_cast, V0_COUNT[J // CH, 2])
                    last = nc.tensor.matmul(ps_l0[s % 2][B % 2], adj_f8[:, J // 2, B * P:(B + 1) * P, J % 2],
                                            v0[:, J, :], start=(J == 0), stop=(J == NB - 1))
                last.then_inc(l0_done, 1)

            for t in range(NT + 3):
                s = t - 3
                if t < NT:
                    turn(2 * t)
                if s >= 0:
                    flip(NT + s, 0, lambda k: cent[:, k, :], NT + s)
                if 1 <= t <= NT:
                    aggregate(2 * t - 1)
                if t < NT:
                    turn(2 * t + 1)
                if s >= 0:
                    if s >= 1:
                        pe.wait_ge(h1_made, 2 * s)
                    else:
                        pe.wait_ge(h0_made, NT)
                    project(NT + s, 0, wx1, E1)
                if t == 0:
                    pe.wait_ge(one_made, 2)
                    pe.wait_ge(hsum_read, 1)
                if t < NT:
                    aggregate(2 * t)

            pe.wait_ge(tr_max, 1)
            nc.tensor.matmul(ps[0:HEADS, 6 * BANK:6 * BANK + P], max4[:, :], ident[:, :],
                             start=True, stop=True).then_inc(tr_pe, 1)
            pe.wait_ge(si_flat_made, 1)
            nc.tensor.transpose(ps[:, 2 * BANK:2 * BANK + P], si_flat, ident[:, :]).then_inc(si_T, 1)
            pe.wait_ge(tr_diag, 1)
            nc.tensor.matmul(ps[:, 7 * BANK:7 * BANK + HEADS], ones[0:HEADS, :], diag4[:, :],
                             start=True, stop=True).then_inc(tr_pe, 1)
            pe.wait_ge(colsum_steps, 2 * NB + 2)
            nc.tensor.matmul(ps[:, 5 * BANK:5 * BANK + D], ones[:, :], colsum[:, :],
                             start=True, stop=True).then_inc(pv_done, 2)
            column_sums(5, hsum1_done)

            pe.wait_ge(siT_made, 1)
            with pe.Fori(0, HEADS) as h:
                for g in range(2):
                    for jt in range(NU):
                        k = jt % 2
                        if g == 0 and jt % (CH // 2) == 0:
                            wait_value(pe, v1_made, h * NCH + jt // (CH // 2) + 1)
                        for b in range(2):
                            if b == 0:
                                wait_value(pe, q_made, h * (2 * NU) + g * NU + jt + 3)
                            else:
                                wait_value(pe, rest_made, h * (2 * NU) + g * NU + jt + 1)
                            for p in range(2):
                                for n in range(GB):
                                    bank = n // 2
                                    first = jt == 0 and b == 0 and p == 0
                                    if first and n % 2 == 0:
                                        wait_value(pe, bank_read, h * (2 * BANKS) + g * BANKS + bank + 1)
                                    at = (n % 2) * 2 * W1 + b * W1
                                    last = nc.tensor.matmul(
                                        ps_acc[:, bank, at:at + W1], q_f8[k][b][:, n * P:(n + 1) * P, p],
                                        v1[:, 2 * jt + p, b, :],
                                        start=(first and n % 2 == 0),
                                        stop=(jt == NU - 1 and b == 1 and p == 1 and n % 2 == 1),
                                        skip_group_check=True)
                                    if jt == NU - 1 and b == 1 and p == 1 and n % 2 == 1 and n < GB - 1:
                                        last.then_inc(bank_done, 1)
                        last.then_inc(pv_done, 1)


_INS = ['x', 'adj', 'L0_gnn_W_fc', 'L0_gnn_b_fc', 'L0_gnn_w_att', 'L0_gnn_b_att',
        'L1_gnn_W', 'L1_gnn_a', 'L1_gnn_gamma', 'L1_gnn_beta']
_OUTS = [((4096, 128), 'float32')]


def kernel(**inputs):
    import numpy as _np
    import concourse.bacc as _bacc
    from concourse import mybir as _mybir
    from concourse.bass_utils import run_bass_kernel_spmd as _run

    nc = _bacc.Bacc("TRN2", target_bir_lowering=False, num_devices=1, dynamic_dma_scratch_size=2048)
    arrays, args = {}, []
    for name in _INS:
        a = _np.ascontiguousarray(inputs[name])
        if name == 'L0_gnn_b_att':
            a = a.reshape(1)
        arrays[f"in_{name}_dram"] = a
        args.append(nc.dram_tensor(f"in_{name}_dram", a.shape, _mybir.dt.from_np(a.dtype), kind="ExternalInput").ap())
    for i, (shape, dtype) in enumerate(_OUTS):
        dt = _mybir.dt.from_np(_np.dtype(dtype))
        args.append(nc.dram_tensor(f"out_{i}_dram", shape, dt, kind="ExternalOutput").ap())
    gnn_two_layers(nc, *args)
    nc.compile()
    r = _run(nc, [arrays], core_ids=[0])
    return r.results[0]["out_0_dram"]
```

```python
import concourse.bass as bass
from concourse import mybir
from contextlib import ExitStack



def gnn_two_layers(nc, x, adj, w_fc, b_fc, w_att, b_att, w1, a1, gamma, beta, out):
    f32 = mybir.dt.float32
    bf16 = mybir.dt.bfloat16
    f16 = mybir.dt.float16
    f8 = mybir.dt.float8e4
    i32 = mybir.dt.int32
    u32 = mybir.dt.uint32
    u16 = mybir.dt.uint16
    i8 = mybir.dt.int8
    u8 = mybir.dt.uint8
    ALU = mybir.AluOpType
    ACT = mybir.ActivationFunctionType
    AX = mybir.AxisListType.X

    N, D = x.shape
    P = 128
    NB = N // P
    NT = NB // 2
    HEADS = 4
    DH = D // HEADS
    C0 = D + 1
    W0 = 3 * C0 + 1
    C1 = DH + 1
    W1 = 3 * C1
    E0, E1 = D + 2, D + 2 * HEADS
    HALF = N // 2
    GB = NB // 2
    EPS = 1e-5
    SLOPE = 0.2
    ONE = 56
    BANK = 512

    x_v = x.rearrange("(t m p) d -> m t (p d)", m=P, p=2)
    out_v = out.rearrange("(t m p) d -> m t (p d)", m=P, p=2)
    adj_v = adj.rearrange("(t m p) j -> t p m j", m=P, p=2)
    x1_dram = nc.dram_tensor("x1_rows", (P, NT, 2 * D), f32, kind="Internal").ap()
    si_dram = nc.dram_tensor("si_rows", (HEADS * NB, P), f32, kind="Internal").ap()

    ctx = ExitStack()
    with ctx:
        def sb(name, shape, dt):
            return ctx.enter_context(nc.sbuf_tensor(name, shape, dt))

        def sem(name):
            return ctx.enter_context(nc.semaphore(name))

        def part(arena, at, shape, dt):
            size = mybir.dt.size(dt)
            n = size
            for k in shape:
                n *= k
            v = arena[:, at:at + n].bitcast(dt)
            if len(shape) == 2:
                v = v.rearrange("p (a b) -> p a b", b=shape[1])
            if len(shape) == 3:
                v = v.rearrange("p (a b c) -> p a b c", b=shape[1], c=shape[2])
            if len(shape) == 4:
                v = v.rearrange("p (a b c d) -> p a b c d", b=shape[1], c=shape[2], d=shape[3])
            return v

        adjT = sb("adjT", [P, NT * N], u16)
        adj_word = adjT[:, :].rearrange("p (t i) -> p t i", i=N)
        adj_u32 = adjT[:, :].bitcast(u32).rearrange("p (t i) -> p t i", i=N // 2)
        adj_f8 = adjT[:, :].bitcast(f8).rearrange("p (t i b) -> p t i b", i=N, b=2)

        hx = sb("hx", [P, NB, E1], f32)

        arena_a = sb("arena_a", [P, 40960], u8)
        stage = [part(arena_a, q * 8192, [HALF], i32) for q in range(4)]
        mask = [part(arena_a, 32768 + q * 2048, [HALF], u8) for q in range(2)]
        sign = part(arena_a, 32768, [HALF], i8)
        words = [part(arena_a, 36864 + q * 2048, [HALF // 2], f16) for q in range(2)]
        srow = [part(arena_a, g * 8192, [HALF], f32) for g in range(2)]
        cmp_i8 = [part(arena_a, 16384 + k * 4096, [HALF, 2], i8) for k in range(2)]
        cmp_u32 = [part(arena_a, 16384 + k * 4096, [HALF // 2], u32) for k in range(2)]
        q_u32 = [[part(arena_a, 24576 + (2 * k + b) * 4096, [HALF // 2], u32) for b in range(2)]
                 for k in range(2)]
        q_f8 = [[part(arena_a, 24576 + (2 * k + b) * 4096, [HALF, 2], f8) for b in range(2)]
                for k in range(2)]

        arena_b = sb("arena_b", [P, NB * W0 * 2], u8)
        v0 = part(arena_b, 0, [NB, W0], bf16)
        v0_parts = v0[:, :, 0:3 * C0].rearrange("p j (c s) -> p j c s", s=3)
        xin = part(arena_b, 0, [NB, D], f32)
        raw0 = part(arena_b, 18432, [NB, 6], f32)
        att_row = part(arena_b, 19200, [2 * D], f32)
        a1_row = part(arena_b, 20224, [2 * DH], f32)
        by_att = [part(arena_b, 20480 + n * 1024, [2, D], f32) for n in range(2)]
        by_a1 = part(arena_b, 22528, [2, HEADS, DH], f32)
        v1 = part(arena_b, 0, [NB, 2, W1], bf16)
        v1_bytes = NB * 2 * W1 * 2
        res = [part(arena_b, v1_bytes + g * GB * 2 * C1 * 4, [GB, 2, C1], f32) for g in range(2)]
        tot = part(arena_b, v1_bytes + 2 * GB * 2 * C1 * 4, [GB, DH], f32)
        at_b = v1_bytes + 2 * GB * 2 * C1 * 4 + GB * C1 * 4
        prod_pool = part(arena_b, at_b, [4, 2, C1], f32)

        arena_c = sb("arena_c", [P, GB * DH * 4], u8)
        xb = part(arena_c, 0, [2, 2, D], f32)
        tmp = part(arena_c, 0, [GB, DH], f32)

        arena_d = sb("arena_d", [P, 2 * E0 * 4], u8)
        wx0 = part(arena_d, 0, [E0], f32)
        bias0 = part(arena_d, E0 * 4, [E0], f32)
        ac = part(arena_d, 0, [HEADS, 2, NB], f32)

        ident = sb("ident", [P, P], f32)
        ident_h = sb("ident_h", [P, P], f16)
        ones = sb("ones", [P, P], f32)
        wx1 = sb("wx1", [P, E1], f32)
        hsum0 = sb("hsum0", [P, D], f32)
        hsum1 = sb("hsum1", [P, HEADS, C1], f32)
        gam = sb("gam", [P, D], f32)
        bet = sb("bet", [P, D], f32)
        agg = sb("agg", [P, 2, C0], f32)
        cent = sb("cent", [P, 2, D], f32)
        hT = sb("hT", [P, 2, D], f32)
        stats = sb("stats", [P, 2, 6], f32)
        mv = sb("mv", [P, NB, 2], f32)
        std = sb("std", [P, NB], f32)
        rstd = sb("rstd", [P, NB], f32)
        bd = sb("bd", [P, HEADS, NB, 2], f32)
        nsj = sb("nsj", [P, HEADS, NB], f32)
        lone = sb("lone", [P, NB], f32)
        fac = sb("fac", [P, NB], f32)
        wj = sb("wj", [P, NB], f32)
        small = sb("small", [P, 16], f32)
        columns = sb("columns", [P, 8], f32)
        eps, neg_half, half_words, max_neg, batt = [columns[:, k:k + 1] for k in range(5)]
        max4 = sb("max4", [P, HEADS], f32)
        diag4 = sb("diag4", [HEADS, HEADS], f32)
        colsum = bd[:, :, :, :].rearrange("p h j k -> p (h j k)")[:, 0:D]
        t_a = cent[:, 0, :].rearrange("p (h b) -> p h b", b=NB)
        t_b = cent[:, 1, :].rearrange("p (h b) -> p h b", b=NB)
        t_c = hT[:, 0, :].rearrange("p (h b) -> p h b", b=NB)
        si_flat = [part(arena_d, 4 * D, [HEADS * GB], f32),
                   agg[:, :, :].rearrange("p k c -> p (k c)")[:, 0:HEADS * GB]]
        siT = [part(arena_d, 0, [P], f32)[0:HEADS * GB, :], hT[0:HEADS * GB, 1, :]]
        den = hT[:, 1, :].rearrange("p (h b) -> p h b", b=NB)

        ps = ctx.enter_context(nc.psum_tensor("ps", [P, 8 * BANK], f32))
        ps_words = [ps[:, k * BANK:(k + 1) * BANK].bitcast(f16) for k in range(2)]
        ps_l0 = [[ps[:, (2 + 2 * u + k) * BANK:(2 + 2 * u + k) * BANK + W0] for k in range(2)]
                 for u in range(2)]
        ps_l0_pair = [ps[:, (2 + 2 * u) * BANK:(4 + 2 * u) * BANK].rearrange("p (k c) -> p k c", k=2)
                      for u in range(2)]
        ps_t = ps[:, 6 * BANK:6 * BANK + 2 * D].rearrange("p (k c) -> p k c", k=2)
        ps_p = ps[:, 7 * BANK:7 * BANK + 2 * E1].rearrange("p (k c) -> p k c", k=2)
        ps_t2 = [ps_t, ps[:, 4 * BANK:4 * BANK + 2 * D].rearrange("p (k c) -> p k c", k=2)]
        ps_p2 = [ps_p, ps[:, 5 * BANK:5 * BANK + 2 * E1].rearrange("p (k c) -> p k c", k=2)]
        hT2 = [hT[:, :, :], cent[:, :, :]]
        ps_si = [ps[0:HEADS * GB, g * 2 * BANK:g * 2 * BANK + P] for g in range(2)]
        ps_acc = ps[:, :].rearrange("p (b c) -> p b c", c=BANK)

        waits_passed = sem("waits_passed")
        X_LOADS = 4
        x_in = [sem(f"x_in{n}") for n in range(X_LOADS)]
        w_in = sem("w_in")
        gb_in = sem("gb_in")
        zeros = sem("zeros")
        consts = sem("consts")
        adj_in = [sem(f"adj_in{q}") for q in range(4)]
        xb_in = [sem(f"xb_in{u}") for u in range(2)]
        x1_stored = [sem(f"x1_stored{u}") for u in range(2)]
        stats_made = sem("stats_made")
        aggr_made = sem("aggr_made")
        wx_products = sem("wx_products")
        neg_mean_made = sem("neg_mean_made")
        cent_act = sem("cent_act")
        wx_made = sem("wx_made")
        std0_made = sem("std0_made")
        rstd0_made = sem("rstd0_made")
        h0_made = sem("h0_made")
        hsum_done = sem("hsum_done")
        hsum_read = sem("hsum_read")
        max_part = sem("max_part")
        max_row = sem("max_row")
        max_one = sem("max_one")
        max_all = sem("max_all")
        neg_made = sem("neg_made")
        fac_steps = sem("fac_steps")
        fac_made = sem("fac_made")
        wj_made = sem("wj_made")
        one_made = sem("one_made")
        v0_rest = sem("v0_rest")
        v0_cast = sem("v0_cast")
        masked = sem("masked")
        masked_act = sem("masked_act")
        colsum_steps = sem("colsum_steps")
        v0_scaled = sem("v0_scaled")
        packed = sem("packed")
        transposed = sem("transposed")
        adj_kept = sem("adj_kept")
        l0_done = sem("l0_done")
        l0_read = sem("l0_read")
        epi = sem("epi")
        x1_made = sem("x1_made")
        mv_made = sem("mv_made")
        std_made = sem("std_made")
        rstd_made = sem("rstd_made")
        cent_made = sem("cent_made")
        cent_T = sem("cent_T")
        hT_made = sem("hT_made")
        proj_done = sem("proj_done")
        h1_made = sem("h1_made")
        tr_max = sem("tr_max")
        tr_diag = sem("tr_diag")
        tr_pe = sem("tr_pe")
        tr_steps = sem("tr_steps")
        bexp_in = sem("bexp_in")
        aexp_in = sem("aexp_in")
        si_flat_made = sem("si_flat_made")
        si_T = sem("si_T")
        exps_made = sem("exps_made")
        siT_made = sem("siT_made")
        si_out = [sem(f"si_out{g}") for g in range(2)]
        srow_in = [sem(f"srow_in{g}") for g in range(2)]
        cmp_act = sem("cmp_act")
        cmp_dve = sem("cmp_dve")
        q_made = sem("q_made")
        rest_made = sem("rest_made")
        q_used = sem("q_used")
        rest_used = sem("rest_used")
        den_made = sem("den_made")
        rden_made = sem("rden_made")
        bank_done = sem("bank_done")
        bank_read = sem("bank_read")
        v1_made = sem("v1_made")
        v1_chain = sem("v1_chain")
        fin_chain = sem("fin_chain")
        head_out = sem("head_out")
        fin_dve = sem("fin_dve")
        o_stats = sem("o_stats")
        o_aggr = sem("o_aggr")
        o_std = sem("o_std")
        o_rstd = sem("o_rstd")
        o_bias_made = sem("o_bias_made")
        o_x1 = [sem(f"o_x1_{k}") for k in range(2)]
        o_xbeta = sem("o_xbeta")
        o_norm = sem("o_norm")
        o_gam = sem("o_gam")
        o_gam_dve = sem("o_gam_dve")
        o_made = sem("o_made")
        o_made_dve = sem("o_made_dve")
        o_out = sem("o_out")

        NU = NT
        BANKS = 8
        EPI = 7
        DVE_Q = (1, 2, 3)
        V1_LINKS = 6
        ACT_PAIR = 1
        DVE_CMPS = NT // 2 - 1
        CH = 4
        NCH = NB // CH
        OG = 4
        NOG = NB // OG
        VECTOR_GROUPS, POOL_GROUPS, SHARED_GROUPS = (NOG // 2, NOG // 2 + 1), (NOG - 1,), (NOG - 2,)
        V0_STEPS = [(c, s) for k in range(NCH + 2) for s in range(3) for c in [k - s] if 0 <= c < NCH]
        V0_COUNT = {cs: n + 1 for n, cs in enumerate(V0_STEPS)}
        V0_RESTS = [cs for cs in V0_STEPS if cs[1] > 0]
        V0_REST_COUNT = {cs: n + 1 for n, cs in enumerate(V0_RESTS)}
        o_x1_half = [part(arena_a, g * 8192, [GB, D], f32) for g in range(2)]
        o_raw = hT[:, 0, 0:GB * 6].rearrange("p (b k) -> p b k", k=6)
        o_bias = fac[:, :]
        wsum = wj[:, :]
        neg_mean = wj[:, :]

        def flat(ap):
            return ap.rearrange("p a c -> p (a c)")

        def row(t3, b, cols=None):
            v = t3[:, bass.ds(b, 1), :] if cols is None else t3[:, bass.ds(b, 1), cols]
            return flat(v)

        def wait_value(eng, signal, value):
            eng.wait_ge(signal, value).then_inc(waits_passed, 1)

        def mean_variance(dve, raw, done, first, count, steps):
            even, odd = raw[:, :, 1], raw[:, :, 4]
            total, gap, gap2 = [cent[:, 0, n * NB:n * NB + count] for n in range(3)]
            mean, var = [mv[:, first:first + count, k] for k in range(2)]
            nc.vector.tensor_tensor(gap, even, odd, ALU.subtract).then_inc(done, 1)
            nc.vector.tensor_tensor(total, even, odd, ALU.add).then_inc(done, 1)
            nc.vector.tensor_tensor(var, raw[:, :, 2], raw[:, :, 5], ALU.add).then_inc(done, 1)
            dve.wait_ge(done, steps + 3)
            nc.vector.tensor_scalar(mean, total, 0.5, None, ALU.mult).then_inc(done, 1)
            nc.vector.tensor_tensor(gap2, gap, gap, ALU.mult).then_inc(done, 1)
            nc.vector.tensor_scalar(var, var, 1.0 / D, None, ALU.mult).then_inc(done, 1)
            dve.wait_ge(done, steps + 6)
            nc.vector.scalar_tensor_tensor(out=var, in0=gap2, scalar=0.25, in1=var,
                                           op0=ALU.mult, op1=ALU.add).then_inc(done, 1)

        def build_v1(eng, waiter, h, c, prod4):
            js = slice(c * CH, (c + 1) * CH)
            dst = v1[:, js].rearrange("p j b (c s) -> p (j b) c s", s=3)
            prod = prod4.rearrange("p j b c -> p (j b) c")
            base = h * (NCH * V1_LINKS) + c * V1_LINKS

            def link(ins, k):
                ins.then_inc(v1_chain, 1)
                wait_value(waiter, v1_chain, base + k)

            if not isinstance(h, int) or c > 0:
                wait_value(waiter, v1_made, h * NCH + c)
            bd_h = bd[:, bass.ds(h, 1), js, :].rearrange("p a j b -> p (a j) b")
            eng.tensor_copy(prod4[:, :, :, DH], bd_h)
            for b in range(2):
                last = eng.tensor_tensor(prod4[:, :, b, 0:DH], hx[:, js, bass.ds(h * DH, DH)],
                                         bd_h[:, :, b].unsqueeze(2).to_broadcast([P, CH, DH]), ALU.mult)
                link(last, b + 1)
            link(eng.tensor_copy(dst[:, :, :, 0], prod), 3)
            link(eng.tensor_tensor(prod, prod, dst[:, :, :, 0], ALU.subtract), 4)
            link(eng.tensor_copy(dst[:, :, :, 1], prod), 5)
            link(eng.tensor_tensor(prod, prod, dst[:, :, :, 1], ALU.subtract), 6)
            eng.tensor_copy(dst[:, :, :, 2], prod).then_inc(v1_made, 1)

        def head_factor(h, k, g):
            return ac[:, bass.ds(h, 1), k, g * GB:(g + 1) * GB].rearrange("p a b -> p (a b)")

        def half_den(h, g):
            return den[:, bass.ds(h, 1), g * GB:(g + 1) * GB].rearrange("p a b -> p (a b)")

        def weights(eng, h, g, link, at):
            d, d2 = half_den(h, g), wsum[:, 0:GB]
            eng.tensor_tensor(d, res[g][:, :, 0, DH], head_factor(h, 0, g), ALU.mult)
            link(eng.tensor_tensor(d2, res[g][:, :, 1, DH], head_factor(h, 1, g), ALU.mult), at + 1)
            eng.tensor_tensor(d, d, d2, ALU.add)
            link(eng.tensor_tensor(wsum[:, GB:NB], lone[:, g * GB:(g + 1) * GB],
                                   hsum1[:, 0, DH:C1].to_broadcast([P, GB]), ALU.mult), at + 2)
            return [eng.tensor_tensor(d, d, wsum[:, GB:NB], ALU.add)]

        def rows_of_head(eng, h, g, link, at):
            blk = slice(g * GB, (g + 1) * GB)
            rden = half_den(h, g)
            lone_factor = wsum[:, 0:GB]
            for k in range(2):
                eng.tensor_tensor(head_factor(h, k, g), head_factor(h, k, g), rden, ALU.mult)
            link(eng.tensor_tensor(lone_factor, lone[:, blk], rden, ALU.mult), at + 1)

            def wide(v):
                return v.unsqueeze(2).to_broadcast([P, GB, DH])

            eng.tensor_tensor(tot, res[g][:, :, 0, 0:DH], wide(head_factor(h, 0, g)), ALU.mult)
            link(eng.tensor_tensor(tmp, res[g][:, :, 1, 0:DH], wide(head_factor(h, 1, g)), ALU.mult), at + 2)
            link(eng.tensor_tensor(tot, tot, tmp, ALU.add), at + 3)
            link(eng.tensor_tensor(tmp, wide(lone_factor),
                                   hsum1[:, bass.ds(h, 1), 0:DH].to_broadcast([P, GB, DH]), ALU.mult), at + 4)
            return [eng.tensor_tensor(hx[:, blk, bass.ds(h * DH, DH)], tot, tmp, ALU.add)]

        def o_rows(n):
            return hx[:, n * OG:(n + 1) * OG, 0:D]

        def o_x1_rows(n):
            return o_x1_half[n // (NOG // 2)][:, n % (NOG // 2) * OG:(n % (NOG // 2) + 1) * OG, :]

        block = ctx.enter_context(nc.Block())

        @block.sync
        def _(sp):
            for n in range(X_LOADS):
                ts = slice(n * NT // X_LOADS, (n + 1) * NT // X_LOADS)
                sp.dma_start(xin.rearrange("p (t q) d -> p t (q d)", q=2)[:, ts], x_v[:, ts]).then_inc(x_in[n], 16)

            def masks_read(t, q):
                if q == 0:
                    sp.wait_ge(masked_act, t)
                else:
                    at = DVE_Q.index(q)
                    sp.wait_ge(masked, t * len(DVE_Q) + at + 1 - len(DVE_Q))

            def body(t, u, has0, has1, has3, half):
                v = 1 - u
                for q in range(4):
                    if has0:
                        if not isinstance(t, int) or t > 0:
                            masks_read(t, q)
                        sp.dma_start(stage[q], adj_v[t, q // 2][:, (q % 2) * HALF:(q % 2 + 1) * HALF])\
                          .then_inc(adj_in[q], 16)
                    if q == 1 and has3:
                        sp.wait_ge(x1_made, t - 2)
                        sp.dma_start(x1_dram[:, t - 3], flat(xb[:, v])).then_inc(x1_stored[v], 16)
                if has1:
                    if has3:
                        wait_value(sp, x1_stored[v], (half if u else half - 1) * 16)
                        sp.wait_ge(cent_made, t + NT - 2)
                    sp.dma_start(flat(xb[:, v]), x_v[:, t - 1]).then_inc(xb_in[v], 16)

            sp.wait_ge(w_in, 16 * 6)
            body(0, 0, True, False, False, 0)
            body(1, 1, True, True, False, 0)
            body(2, 0, True, True, False, 1)
            body(3, 1, True, True, True, 1)
            with sp.Fori(2, NT // 2) as half:
                body(half * 2, 0, True, True, True, half)
                body(half * 2 + 1, 1, True, True, True, half)
            body(NT, 0, False, True, True, NT // 2)

            si_v = si_dram.rearrange("(g h b) m -> h g (b m)", h=HEADS, g=2)

            def rows(h, g):
                sp.dma_start(srow[g], si_v[h, g].partition_broadcast(P)).then_inc(srow_in[g], 16)

            def first_rows(g):
                masks_read(NT, g)
                sp.wait_ge(siT_made, g + 1)
                n = HEADS * GB
                sp.dma_start(si_dram[g * n:(g + 1) * n], siT[g]).then_inc(si_out[g], 16)
                sp.wait_ge(si_out[g], 16)
                rows(0, g)

            first_rows(0)
            body(NT + 1, 1, False, False, True, NT // 2)
            body(NT + 2, 0, False, False, True, NT // 2 + 1)
            first_rows(1)

            with sp.Fori(1, HEADS) as h:
                for g in range(2):
                    wait_value(sp, cmp_act, h * (2 * NU) + (g + 1 - 2) * NU)
                    wait_value(sp, cmp_dve, h * (2 * DVE_CMPS) + (g + 1 - 2) * DVE_CMPS)
                    rows(h, g)

            for u in range(2):
                sp.wait_ge(x1_stored[u], 16 * (NT // 2))
            for g in range(2):
                sp.wait_ge(cmp_act, (2 * HEADS - 1 + g) * NU)
                sp.wait_ge(cmp_dve, (2 * HEADS - 1 + g) * DVE_CMPS)
                sp.dma_start(o_x1_half[g].rearrange("p (t q) d -> p t (q d)", q=2),
                             x1_dram[:, g * (GB // 2):(g + 1) * (GB // 2)]).then_inc(o_x1[g], 16)

            def store(n):
                sp.dma_start(out_v[:, n * (OG // 2):(n + 1) * (OG // 2)],
                             o_x1_rows(n).rearrange("m (t p) d -> m t (p d)", p=2)).then_inc(o_out, 16)

            for n in range(NOG // 2):
                sp.wait_ge(o_made, n + 1)
                store(n)
            sp.wait_ge(o_made_dve, 1)
            store(VECTOR_GROUPS[0])
            for n in POOL_GROUPS:
                sp.wait_ge(o_made, NOG // 2 + 1 + POOL_GROUPS.index(n))
                store(n)
            for k, n in enumerate((*VECTOR_GROUPS[1:], *SHARED_GROUPS)):
                sp.wait_ge(o_made_dve, k + 2)
                store(n)
            sp.wait_ge(o_out, 16 * NOG)

        @block.gpsimd
        def _(pool):
            nc.gpsimd.memset(ident[:, :], 0.0).then_inc(zeros, 1)
            nc.gpsimd.memset(ident_h[:, :], 0.0).then_inc(zeros, 1)
            nc.gpsimd.memset(ones[:, :], 1.0).then_inc(consts, 1)
            nc.gpsimd.memset(eps[:, :], EPS).then_inc(consts, 1)
            nc.gpsimd.memset(neg_half[:, :], -0.5).then_inc(consts, 1)
            nc.gpsimd.memset(half_words[:, :], 257.0 * ONE / 2).then_inc(consts, 1)
            nc.gpsimd.memset(hsum1[:, :, DH:C1], float(N)).then_inc(head_out, 2)
            pool.wait_ge(zeros, 2)
            for m in (ident, ident_h):
                nc.gpsimd.affine_select(out=m[:, :], in_=m[:, :], compare_op=ALU.not_equal, fill=1.0,
                                        base=0, pattern=[[-1, P]], channel_multiplier=1).then_inc(consts, 1)

            def add_to_colsum(B, k):
                nc.gpsimd.tensor_tensor(colsum[:, :], colsum[:, :], row(hx, B, slice(0, D)), ALU.add)\
                    .then_inc(colsum_steps, 1)
                wait_value(pool, colsum_steps, k)

            nc.gpsimd.memset(colsum[:, :], 0.0).then_inc(colsum_steps, 1)
            pool.wait_ge(colsum_steps, 1)
            for t in range(NT):
                pool.wait_ge(h0_made, t + 1)
                for k in range(2):
                    add_to_colsum(2 * t + k, 2 * t + k + 2)
            pool.wait_ge(one_made, 2)
            pool.wait_ge(wj_made, 1)
            for c in range(NCH):
                js = slice(c * CH, (c + 1) * CH)
                nc.gpsimd.tensor_tensor(hx[:, js, 0:C0], hx[:, js, 0:C0],
                                        wj[:, js].unsqueeze(2).to_broadcast([P, CH, C0]), ALU.mult)\
                    .then_inc(v0_scaled, 1)
            pool.wait_ge(hsum_done, 1)
            nc.gpsimd.memset(colsum[:, :], 0.0).then_inc(colsum_steps, 1)
            pool.wait_ge(colsum_steps, NB + 2)

            def sums(s):
                wait_value(pool, h1_made, s * 2 + 2)
                for k in range(2):
                    add_to_colsum(s * 2 + k, s * 2 + (k + NB + 3))

            with pool.Fori(0, NT) as s:
                sums(s)

            FIN = 6

            def link_of(h, g):
                def link(ins, k):
                    ins.then_inc(fin_chain, 1)
                    wait_value(pool, fin_chain, (h * 2 + g) * FIN + k)
                return link

            def pool_weights(h, g):
                wait_value(pool, bank_read, (h * 2 + g + 2) * BANKS)
                wait_value(pool, head_out, h * 2 + g + 2)
                weights(nc.gpsimd, h, g, link_of(h, g), 0)[0].then_inc(den_made, 1)

            def pool_rows(h, g):
                wait_value(pool, rden_made, h * 2 + g + 1)
                rows_of_head(nc.gpsimd, h, g, link_of(h, g), 2)[0].then_inc(head_out, 1)

            pool.wait_ge(exps_made, 4)
            for c in range(1, NCH):
                build_v1(nc.gpsimd, pool, 0, c, prod_pool)
            with pool.Fori(0, HEADS - 1) as h:
                pool_weights(h, 0)
                for c in range(NCH):
                    wait_value(pool, rest_used, h * (2 * NU) + NU + (c + 1) * (CH // 2) + 2)
                    build_v1(nc.gpsimd, pool, h + 1, c, prod_pool)
                pool_rows(h, 0)
                pool_weights(h, 1)
                pool_rows(h, 1)
            pool_weights(HEADS - 1, 0)
            pool_rows(HEADS - 1, 0)

            pool.wait_ge(gb_in, 32)
            for n in range(NOG):
                if n % (NOG // 2) == 0:
                    pool.wait_ge(o_x1[n // (NOG // 2)], 16)
                nc.gpsimd.tensor_tensor(o_x1_rows(n), o_x1_rows(n),
                                        bet[:, :].unsqueeze(1).to_broadcast([P, OG, D]), ALU.add)\
                    .then_inc(o_xbeta, 1)
            pool.wait_ge(o_xbeta, NOG)
            for k, n in enumerate((*range(NOG // 2), *POOL_GROUPS)):
                pool.wait_ge(o_norm, k + 1)
                nc.gpsimd.tensor_tensor(o_rows(n), o_rows(n), gam[:, :].unsqueeze(1).to_broadcast([P, OG, D]),
                                        ALU.mult).then_inc(o_gam, 1)
                pool.wait_ge(o_gam, k + 1)
                nc.gpsimd.tensor_tensor(o_x1_rows(n), o_rows(n), o_x1_rows(n), ALU.add).then_inc(o_made, 1)

        @block.scalar
        def _(act):
            act.dma_start(wx0[:, 0:D], w_fc).then_inc(w_in, 16)
            act.dma_start(wx1[:, 0:D], w1).then_inc(w_in, 16)
            act.dma_start(att_row, w_att.partition_broadcast(P)).then_inc(w_in, 16)
            act.dma_start(a1_row, a1.rearrange("n o -> (n o)").partition_broadcast(P)).then_inc(w_in, 16)
            act.dma_start(bias0[:, 0:D], b_fc.partition_broadcast(P)).then_inc(w_in, 16)
            act.dma_start(batt[:, :], b_att.partition_broadcast(P)).then_inc(w_in, 16)
            act.dma_start(gam[:, :], gamma.partition_broadcast(P)).then_inc(gb_in, 16)
            act.dma_start(bet[:, :], beta.partition_broadcast(P)).then_inc(gb_in, 16)

            act.wait_ge(consts, 6)

            def keep(t, q):
                act.wait_ge(transposed, t * 4 + q + 1)
                to = adj_word[:, (q % 2) * (NT // 2):(q % 2 + 1) * (NT // 2),
                              bass.ds(t * (2 * P) + (q // 2) * P, P)]
                of = ps_words[q % 2].rearrange("p (a m) -> p a m", m=P)
                if q == 0:
                    nc.scalar.activation(to, of, ACT.Identity, scale=float(ONE) / 2,
                                         bias=half_words[:, :]).then_inc(adj_kept, 1)
                else:
                    nc.scalar.activation(to, of, ACT.Copy, scale=float(ONE)).then_inc(adj_kept, 1)

            def compare(t):
                if not isinstance(t, int) or t > 0:
                    act.wait_ge(packed, t * 4 - 1)
                act.wait_ge(adj_in[0], t * 16 + 16)
                nc.scalar.activation(sign, stage[0], ACT.Sign, bias=neg_half[:, :]).then_inc(masked_act, 1)

            act.wait_ge(aggr_made, 7)
            nc.scalar.activation(std[:, :], mv[:, :, 1], ACT.Sqrt, bias=eps[:, :]).then_inc(std0_made, 1)
            compare(0)
            def copy_turned(t, u, free):
                act.wait_ge(cent_T, t + 1)
                if free:
                    act.wait_ge(proj_done, t - 1)
                nc.scalar.activation(hT2[u], ps_t2[u], ACT.Copy).then_inc(hT_made, 1)

            act.wait_ge(neg_mean_made, 1)
            for t in range(NT):
                if t < NT // 2:
                    for B in (NT + 2 * t, NT + 2 * t + 1):
                        last = nc.scalar.activation(xin[:, B, :], xin[:, B, :], ACT.Relu,
                                                    bias=neg_mean[:, B:B + 1])
                    last.then_inc(cent_act, 1)
                copy_turned(t, t % 2, t >= 2)
                if t == 11:
                    keep(0, 0)
                if t == 12:
                    keep(0, 1)
            keep(0, 2)
            compare(1)
            keep(0, 3)
            act.wait_ge(neg_made, 1)
            nc.scalar.activation(wj[:, :], hx[:, :, D + 1], ACT.Exp, bias=max_neg[:, :]).then_inc(wj_made, 1)
            act.wait_ge(fac_made, 1)
            nc.scalar.activation(fac[:, :], fac[:, :], ACT.Exp).then_inc(wj_made, 1)
            for c, s in V0_STEPS:
                js = slice(c * CH, (c + 1) * CH)
                if s == 0:
                    act.wait_ge(v0_scaled, c + 1)
                else:
                    act.wait_ge(v0_rest, V0_REST_COUNT[c, s])
                nc.scalar.activation(v0_parts[:, js, :, s], hx[:, js, 0:C0], ACT.Copy).then_inc(v0_cast, 1)

            def body(t, u, has0, has3, ahead=True):
                v = 1 - u
                if has3:
                    act.wait_ge(mv_made, t - 2)
                    nc.scalar.activation(std[:, 0:2], mv[:, 0:2, 1], ACT.Sqrt, bias=eps[:, :])\
                        .then_inc(std_made, 1)
                if has0:
                    keep(t, 0)
                    keep(t, 1)
                if has3:
                    act.wait_ge(cent_T, t + (NT - 2))
                    nc.scalar.activation(hT[:, :, :], ps_t, ACT.Copy).then_inc(hT_made, 1)
                if ahead:
                    compare(t + 1)
                if has0:
                    keep(t, 2)
                    keep(t, 3)
                if has3:
                    act.wait_ge(proj_done, t + (NT - 2))
                    act.wait_ge(rstd_made, t - 2)
                    for k in range(2):
                        nc.scalar.activation(row(hx, t * 2 + (k - 6)), ps_p[:, k, :], ACT.Copy,
                                             scale=rstd[:, 2 * v + k:2 * v + k + 1]).then_inc(h1_made, 1)

            body(1, 1, True, False)
            body(2, 0, True, False)
            body(3, 1, True, True)
            with act.Fori(2, NT // 2 - 1) as half:
                body(half * 2, 0, True, True)
                body(half * 2 + 1, 1, True, True)
            body(NT - 2, 0, True, True)
            body(NT - 1, 1, True, True, False)
            def copy_si(g):
                act.wait_ge(si_T, g + 1)
                nc.scalar.activation(siT[g], ps_si[g], ACT.Copy).then_inc(siT_made, 1)

            body(NT, NT % 2, False, True, False)
            copy_si(0)
            for t in range(NT + 1, NT + 3):
                body(t, t % 2, False, True, False)

            def compare_unit(h, g, jj, k):
                used = h * (2 * NU) + g * NU + jj * 2 + k + 1
                if isinstance(jj, int):
                    wait_value(act, q_made, used)
                else:
                    act.wait_ge(q_made, used)
                both = k == 0 or (isinstance(jj, int) and jj == ACT_PAIR)
                for p in range(2 if both else 1):
                    last = nc.scalar.activation(
                        cmp_i8[k][:, :, p], srow[g], ACT.Sign, scale=-1.0,
                        bias=row(nsj, h, bass.ds(jj * 4 + 2 * k + p, 1)))
                last.then_inc(cmp_act, 1)

            act.wait_ge(srow_in[0], 16)
            compare_unit(0, 0, 0, 0)

            act.wait_ge(bexp_in, 1)
            act.wait_ge(rest_used, 2)
            for k, slope in enumerate((1.0, SLOPE)):
                nc.scalar.activation(bd[:, :, :, k], t_a, ACT.Exp, scale=slope).then_inc(exps_made, 1)
            copy_si(1)
            act.wait_ge(si_out[0], 16)
            act.wait_ge(aexp_in, 2)
            for k, t_k in enumerate((t_b, t_c)):
                nc.scalar.activation(ac[:, :, k, :], t_k, ACT.Exp).then_inc(exps_made, 1)

            def compare_pairs(h, g, first):
                wait_value(act, srow_in[g], h * 16 + 16)
                for jj in range(first, ACT_PAIR + 1):
                    compare_unit(h, g, jj, 0)
                    compare_unit(h, g, jj, 1)
                with act.Fori((ACT_PAIR + 1) // 2, NU // 4) as two:
                    for n in range(2):
                        compare_unit(h, g, two * 2 + n, 0)
                        compare_unit(h, g, two * 2 + n, 1)

            compare_unit(0, 0, 0, 1)
            compare_pairs(0, 0, 1)
            compare_pairs(0, 1, 0)
            with act.Fori(1, HEADS) as h:
                for g in range(2):
                    compare_pairs(h, g, 0)

            for g in range(2):
                blk = slice(g * GB, (g + 1) * GB)
                act.wait_ge(o_aggr, 7 * (g + 1))
                nc.scalar.activation(std[:, blk], mv[:, blk, 1], ACT.Sqrt, bias=eps[:, :]).then_inc(o_std, 1)
                act.wait_ge(o_bias_made, g + 1)
                for n in (POOL_GROUPS + SHARED_GROUPS if g else range(NOG // 2)):
                    for B in range(n * OG, (n + 1) * OG):
                        last = nc.scalar.activation(hx[:, B, 0:D], hx[:, B, 0:D], ACT.Identity,
                                                    scale=rstd[:, B:B + 1], bias=o_bias[:, B:B + 1])
                    last.then_inc(o_norm, 1)

        @block.vector
        def _(dve):
            for b in range(NB):
                if b % (NB // X_LOADS) == 0:
                    dve.wait_ge(x_in[b // (NB // X_LOADS)], 16)
                nc.vector.bn_stats(raw0[:, b, :], xin[:, b, :]).then_inc(stats_made, 1)
            dve.wait_ge(stats_made, NB)
            mean_variance(dve, raw0, aggr_made, 0, NB, 0)
            dve.wait_ge(aggr_made, 7)
            nc.vector.tensor_scalar(neg_mean, mv[:, :, 0], -1.0, None, ALU.mult).then_inc(neg_mean_made, 1)
            dve.wait_ge(w_in, 16 * 6)
            dve.wait_ge(consts, 6)
            att = att_row.rearrange("p (k d) -> p k d", k=2)
            for to, w in zip(by_att, (wx0, bias0)):
                nc.vector.tensor_tensor(to, w[:, 0:D].unsqueeze(1).to_broadcast([P, 2, D]), att, ALU.mult)\
                    .then_inc(wx_products, 1)
            nc.vector.tensor_tensor(
                by_a1, wx1[:, 0:D].rearrange("p (h d) -> p h d", d=DH).unsqueeze(1).to_broadcast([P, 2, HEADS, DH]),
                a1_row.rearrange("p (k d) -> p k d", k=2).unsqueeze(2).to_broadcast([P, 2, HEADS, DH]),
                ALU.mult).then_inc(wx_products, 1)
            dve.wait_ge(wx_products, 3)
            nc.vector.tensor_reduce(wx0[:, D:E0], by_att[0], AX, ALU.add)
            nc.vector.tensor_reduce(bias0[:, D:E0], by_att[1], AX, ALU.add)
            nc.vector.tensor_reduce(wx1[:, D:E1].rearrange("p (k h) -> p k h", k=2), by_a1, AX, ALU.add)\
                .then_inc(wx_made, 1)
            for t in range(NT // 2):
                for B in (2 * t, 2 * t + 1):
                    last = nc.vector.tensor_scalar(xin[:, B, :], xin[:, B, :], mv[:, B, 0:1], 0.0,
                                                   ALU.subtract, ALU.max)
                last.then_inc(cent_made, 2)
            dve.wait_ge(std0_made, 1)
            nc.vector.reciprocal(rstd[:, :], std[:, :]).then_inc(rstd0_made, 1)
            dve.wait_ge(rstd0_made, 1)
            dve.wait_ge(wx_made, 1)

            def compare(t, q):
                if not isinstance(t, int) or 4 * t + q >= 2:
                    dve.wait_ge(packed, t * 4 + q - 1)
                dve.wait_ge(adj_in[q], t * 16 + 16)
                nc.vector.tensor_scalar(mask[q % 2], stage[q], 0.0, None, ALU.is_gt).then_inc(masked, 1)

            def pack(t, q):
                if q == 0:
                    dve.wait_ge(masked_act, t + 1)
                else:
                    dve.wait_ge(masked, t * len(DVE_Q) + DVE_Q.index(q) + 1)
                if not isinstance(t, int) or 4 * t + q >= 2:
                    dve.wait_ge(transposed, t * 4 + q - 1)
                pair = (sign if q == 0 else mask[q % 2]).rearrange("p (w b) -> p w b", b=2)
                nc.vector.scalar_tensor_tensor(out=words[q % 2], in0=pair[:, :, 1], scalar=256.0,
                                               in1=pair[:, :, 0], op0=ALU.mult, op1=ALU.add)\
                    .then_inc(packed, 1)

            def scaled(t, u):
                dve.wait_ge(proj_done, t + 1)
                for k in range(2):
                    last = nc.vector.scalar_tensor_tensor(
                        out=row(hx, t * 2 + k, slice(0, E0)), in0=ps_p2[u][:, k, 0:E0],
                        scalar=rstd[:, bass.ds(t * 2 + k, 1)], in1=bias0[:, :], op0=ALU.mult, op1=ALU.add)
                last.then_inc(h0_made, 1)

            first_block = {1: (compare, 1), 2: (pack, 0), 3: (pack, 1), 4: (compare, 2), 5: (compare, 3),
                           6: (pack, 2), 7: (pack, 3)}
            for t in range(NT):
                scaled(t, t % 2)
                if t % 2 and t // 2 in first_block:
                    step, q = first_block[t // 2]
                    step(0, q)
            dve.wait_ge(h0_made, NT)

            nc.vector.reduce_max(small[:, 0:1], hx[:, :, D + 1], AX).then_inc(max_part, 1)
            nc.vector.tensor_scalar(fac[:, :], hx[:, :, D], batt[:, :], None, ALU.add).then_inc(fac_steps, 1)
            dve.wait_ge(max_row, 1)
            nc.vector.reduce_max(small[0:1, 2:3], ps[0:1, 6 * BANK:6 * BANK + P], AX).then_inc(max_one, 1)
            dve.wait_ge(max_all, 1)
            nc.vector.tensor_scalar(max_neg[:, :], ps[:, 7 * BANK:7 * BANK + 1], -1.0, None, ALU.mult)\
                .then_inc(neg_made, 1)
            dve.wait_ge(neg_made, 1)
            dve.wait_ge(fac_steps, 1)
            nc.vector.tensor_scalar(std[:, :], fac[:, :], max_neg[:, :], None, ALU.subtract)\
                .then_inc(fac_steps, 1)
            dve.wait_ge(fac_steps, 2)
            nc.vector.scalar_tensor_tensor(out=fac[:, :], in0=fac[:, :], scalar=max_neg[:, :],
                                           in1=std[:, :], op0=ALU.subtract, op1=ALU.subtract)\
                .then_inc(fac_made, 1)
            nc.vector.memset(hx[:, :, D:C0], 1.0).then_inc(one_made, 1)
            nc.vector.memset(v0[:, :, W0 - 1:W0], 1.0).then_inc(one_made, 1)
            dve.wait_ge(hsum_done, 1)
            nc.vector.tensor_copy(hsum0[:, :], ps[:, 3 * BANK:3 * BANK + D]).then_inc(hsum_read, 1)
            for c, s in V0_RESTS:
                js = slice(c * CH, (c + 1) * CH)
                dve.wait_ge(v0_cast, V0_COUNT[c, s - 1])
                nc.vector.tensor_tensor(hx[:, js, 0:C0], hx[:, js, 0:C0], v0_parts[:, js, :, s - 1],
                                        ALU.subtract).then_inc(v0_rest, 1)
            dve.wait_ge(wj_made, 2)

            def take(t, u, has0, has2, has3, half):
                s, v = t - 2, 1 - u

                two = bass.ds(t * 2 - 4, 2)

                def made(k):
                    dve.wait_ge(epi, t * EPI + (k - 2 * EPI))

                def step_sum():
                    dve.wait_ge(l0_done, t * 2 - 2)
                    nc.vector.tensor_reduce(
                        agg[:, :, :], ps_l0_pair[u][:, :, 0:3 * C0].rearrange("p k (c s) -> p k c s", s=3),
                        AX, ALU.add).then_inc(epi, 1)
                    nc.vector.tensor_scalar(lone[:, two], ps_l0_pair[u][:, :, W0 - 1], 0.0, None, ALU.is_equal)\
                        .then_inc(l0_read, 1)

                def step_weight():
                    made(1)
                    nc.vector.tensor_tensor(small[:, 0:2], agg[:, :, D], fac[:, two], ALU.mult).then_inc(epi, 1)

                def step_count():
                    made(2)
                    dve.wait_ge(l0_read, t - 1)
                    nc.vector.scalar_tensor_tensor(out=small[:, 2:4], in0=lone[:, two], scalar=float(N),
                                                   in1=small[:, 0:2], op0=ALU.mult, op1=ALU.add)\
                        .then_inc(epi, 1)

                def step_reciprocal():
                    made(3)
                    nc.vector.reciprocal(small[:, 4:6], small[:, 2:4]).then_inc(epi, 1)

                def step_factors():
                    made(4)
                    nc.vector.tensor_tensor(small[:, 6:8], fac[:, two], small[:, 4:6], ALU.mult)
                    nc.vector.tensor_tensor(small[:, 8:10], lone[:, two], small[:, 4:6], ALU.mult)\
                        .then_inc(epi, 1)

                def step_rows():
                    made(5)
                    dve.wait_ge(xb_in[u], half * 16)
                    for k in range(2):
                        last = nc.vector.scalar_tensor_tensor(
                            out=xb[:, u, k, :], in0=agg[:, k, 0:D], scalar=small[:, 6 + k:7 + k],
                            in1=xb[:, u, k, :], op0=ALU.mult, op1=ALU.add)
                    last.then_inc(epi, 1)

                def step_lone_rows():
                    made(6)
                    for k in range(2):
                        last = nc.vector.scalar_tensor_tensor(
                            out=xb[:, u, k, :], in0=hsum0[:, :], scalar=small[:, 8 + k:9 + k],
                            in1=xb[:, u, k, :], op0=ALU.mult, op1=ALU.add)
                    last.then_inc(x1_made, 1)

                def step_statistics():
                    dve.wait_ge(x1_made, t - 1)
                    for k in range(2):
                        last = nc.vector.bn_stats(stats[:, k, :], xb[:, u, k, :])
                    last.then_inc(epi, 1)
                    wait_value(dve, epi, t * EPI + (7 - 2 * EPI))
                    for k in range(2):
                        last = nc.vector.bn_aggr(mv[:, k, :], stats[:, k, :])
                    last.then_inc(mv_made, 1)

                def center_rstd():
                    dve.wait_ge(std_made, t - 2)
                    if not isinstance(t, int) or t > 3:
                        dve.wait_ge(hT_made, t + (NT - 3))
                    nc.vector.reciprocal(rstd[:, 2 * v:2 * v + 2], std[:, 0:2]).then_inc(rstd_made, 1)

                def center_rows():
                    dve.wait_ge(mv_made, t - 2)
                    if not isinstance(t, int) or t > 3:
                        dve.wait_ge(cent_T, t + (NT - 3))
                    for k in range(2):
                        last = nc.vector.tensor_scalar(cent[:, k, :], xb[:, v, k, :], mv[:, k, 0:1], 0.0,
                                                       ALU.subtract, ALU.max)
                    last.then_inc(cent_made, 1)

                if has0:
                    compare(t, 1)
                if has3:
                    center_rows()
                    center_rstd()
                if has0:
                    pack(t, 0)
                if has2:
                    step_sum()
                if has0:
                    pack(t, 1)
                if has2:
                    step_weight()
                if has0:
                    compare(t, 2)
                if has2:
                    step_count()
                if has0:
                    compare(t, 3)
                if has2:
                    step_reciprocal()
                    step_factors()
                if has0:
                    pack(t, 2)
                if has2:
                    step_rows()
                if has0:
                    pack(t, 3)
                if has2:
                    step_lone_rows()
                    step_statistics()

            take(1, 1, True, False, False, 0)
            take(2, 0, True, True, False, 1)
            take(3, 1, True, True, True, 1)
            with dve.Fori(2, NT // 2) as half:
                take(half * 2, 0, True, True, True, half)
                take(half * 2 + 1, 1, True, True, True, half)
            def flatten_si(g):
                dve.wait_ge(h1_made, (g + 1) * NT)
                nc.vector.tensor_copy(si_flat[g].rearrange("p (h j) -> p h j", j=GB),
                                      hx[:, g * GB:(g + 1) * GB, D:D + HEADS].rearrange("p j h -> p h j"))\
                    .then_inc(si_flat_made, 1)

            flatten_si(0)
            take(NT, 0, False, True, True, NT // 2)
            take(NT + 1, 1, False, True, True, NT // 2)
            take(NT + 2, 0, False, False, True, NT // 2 + 1)

            dve.wait_ge(h1_made, 2 * NT)
            si = hx[:, :, D:D + HEADS].rearrange("p j h -> p h j")
            sj = hx[:, :, D + HEADS:E1].rearrange("p j h -> p h j")
            nc.vector.reduce_max(max4[:, :], sj, AX).then_inc(tr_max, 1)
            flatten_si(1)
            nc.vector.tensor_scalar(nsj[:, :, :], sj, -1.0, None, ALU.mult).then_inc(q_made, 2)
            nc.vector.memset(small[:, 15:16], 0.0).then_inc(rest_made, 2)
            dve.wait_ge(q_made, 2)
            dve.wait_ge(tr_pe, 1)
            nc.vector.reduce_max(small[0:HEADS, 0:1], ps[0:HEADS, 6 * BANK:6 * BANK + P], AX)\
                .then_inc(tr_steps, 1)
            dve.wait_ge(tr_steps, 1)
            nc.vector.tensor_scalar(diag4[:, :], ident[0:HEADS, 0:HEADS], small[0:HEADS, 0:1], None, ALU.mult)\
                .then_inc(tr_diag, 1)
            dve.wait_ge(tr_pe, 2)
            nc.vector.tensor_copy(max4[:, :], ps[:, 7 * BANK:7 * BANK + HEADS]).then_inc(tr_steps, 1)
            dve.wait_ge(tr_steps, 2)
            wide = max4[:, :].unsqueeze(2).to_broadcast([P, HEADS, NB])
            nc.vector.tensor_tensor(t_a, sj, wide, ALU.subtract).then_inc(bexp_in, 1)
            nc.vector.tensor_tensor(t_b, si, wide, ALU.add).then_inc(tr_steps, 1)
            dve.wait_ge(tr_steps, 3)
            row_max = xb[:, 0].rearrange("p k d -> p (k d)")[:, 0:HEADS * NB].rearrange("p (h j) -> p h j", j=NB)
            dve.wait_ge(x1_stored[0], 16 * (NT // 2))
            nc.vector.scalar_tensor_tensor(out=row_max, in0=t_b, scalar=SLOPE, in1=t_b, op0=ALU.mult,
                                           op1=ALU.max).then_inc(tr_steps, 1)
            dve.wait_ge(tr_steps, 4)
            nc.vector.scalar_tensor_tensor(out=t_c, in0=t_b, scalar=SLOPE, in1=row_max, op0=ALU.mult,
                                           op1=ALU.subtract).then_inc(aexp_in, 1)
            dve.wait_ge(aexp_in, 1)
            nc.vector.tensor_tensor(t_b, t_b, row_max, ALU.subtract).then_inc(aexp_in, 1)
            dve.wait_ge(rest_used, 2)
            nc.vector.tensor_copy(hsum1[:, :, 0:DH], ps[:, 5 * BANK:5 * BANK + D]
                                  .rearrange("p (h d) -> p h d", d=DH)).then_inc(bank_read, BANKS)

            def adjacency(g, jj, k):
                return flat(adj_u32[:, bass.ds(jj * 2 + k, 1), g * (HALF // 2):(g + 1) * (HALF // 2)])

            def front(h, g, jj, between=None):
                u = h * (2 * NU) + g * NU + jj * 2
                ours = not (isinstance(jj, int) and jj == ACT_PAIR)
                if ours:
                    dve.wait_ge(q_made, u + 2)
                    nc.vector.tensor_scalar(cmp_i8[1][:, :, 1], srow[g], row(nsj, h, bass.ds(jj * 4 + 3, 1)),
                                            float(ONE), ALU.is_gt, ALU.mult).then_inc(cmp_dve, 1)
                for k in range(2):
                    dve.wait_ge(cmp_act, u + k + 1)
                    if k == 1 and ours:
                        first = isinstance(jj, int) and jj < ACT_PAIR
                        dve.wait_ge(cmp_dve, h * (2 * DVE_CMPS) + (g * DVE_CMPS + (1 if first else 0)) + jj)
                    dve.wait_ge(q_used, u + k + 1)
                    dve.wait_ge(rest_made, u + k + 1)
                    nc.vector.tensor_tensor(q_u32[k][0], cmp_u32[k], adjacency(g, jj, k), ALU.bitwise_and)\
                        .then_inc(q_made, 1)
                    if k == 0 and between:
                        between()

            def back(h, g, jj):
                u = h * (2 * NU) + g * NU + jj * 2
                for k in range(2):
                    dve.wait_ge(q_made, u + k + 3)
                    dve.wait_ge(rest_used, u + k + 1)
                    nc.vector.tensor_tensor(q_u32[k][1], q_u32[k][0], adjacency(g, jj, k), ALU.bitwise_xor)\
                        .then_inc(rest_made, 1)

            def sums(h, g):
                wait_value(dve, head_out, h * 2 + g + 1)
                for n in range(BANKS):
                    if n < BANKS - 1:
                        dve.wait_ge(bank_done, h * (2 * BANKS - 2) + g * (BANKS - 1) + n + 1)
                    else:
                        dve.wait_ge(rest_used, h * (2 * NU) + (g + 1) * NU + 2)
                    nc.vector.tensor_reduce(
                        res[g][:, 2 * n:2 * n + 2].rearrange("p a b c -> p (a b c)"),
                        ps_acc[:, n, 0:4 * W1].rearrange("p (c s) -> p c s", s=3), AX, ALU.add)\
                        .then_inc(bank_read, 1)

            def invert(h, g):
                wait_value(dve, den_made, h * 2 + g + 1)
                d = den[:, bass.ds(h, 1), g * GB:(g + 1) * GB].rearrange("p a b -> p (a b)")
                nc.vector.reciprocal(d, d).then_inc(rden_made, 1)

            def start_pass(h, g):
                wait_value(dve, srow_in[g], h * 16 + 16)
                front(h, g, 0)

            def pairs(h, g, first, last):
                if first == ACT_PAIR:
                    front(h, g, first)
                    back(h, g, first)
                    first += 1
                with dve.Fori(first // 2, last // 2) as two:
                    for n in range(2):
                        front(h, g, two * 2 + n)
                        back(h, g, two * 2 + n)

            def first_chunk():
                dve.wait_ge(exps_made, 2)
                build_v1(nc.vector, dve, 0, 0, prod_pool)

            dve.wait_ge(srow_in[0], 16)
            front(0, 0, 0, first_chunk)
            back(0, 0, 0)
            pairs(0, 0, 1, NU // 2)
            start_pass(0, 1)
            sums(0, 0)
            with dve.Fori(1, HEADS) as h:
                back(h - 1, 1, 0)
                pairs(h - 1, 1, 1, NU // 2)
                invert(h - 1, 0)
                start_pass(h, 0)
                sums(h - 1, 1)
                back(h, 0, 0)
                pairs(h, 0, 1, NU // 2)
                invert(h - 1, 1)
                start_pass(h, 1)
                sums(h, 0)
            H = HEADS - 1
            back(H, 1, 0)
            pairs(H, 1, 1, 4)
            invert(H, 0)
            pairs(H, 1, 4, 6)
            def statistics(g):
                for n in range(GB):
                    last = nc.vector.bn_stats(o_raw[:, n, :], hx[:, g * GB + n, 0:D])
                last.then_inc(o_stats, 1)
                dve.wait_ge(o_stats, g + 1)
                mean_variance(dve, o_raw, o_aggr, g * GB, GB, 7 * g)

            def scales(g):
                blk = slice(g * GB, (g + 1) * GB)
                dve.wait_ge(o_std, g + 1)
                nc.vector.reciprocal(rstd[:, blk], std[:, blk]).then_inc(o_rstd, 1)
                dve.wait_ge(o_rstd, g + 1)
                nc.vector.scalar_tensor_tensor(out=o_bias[:, blk], in0=mv[:, blk, 0], scalar=-1.0,
                                               in1=rstd[:, blk], op0=ALU.mult, op1=ALU.mult)\
                    .then_inc(o_bias_made, 1)

            dve.wait_ge(head_out, 2 * HEADS + 1)
            statistics(0)
            pairs(H, 1, 6, NU // 2)
            scales(0)
            sums(H, 1)

            def link(ins, k):
                ins.then_inc(fin_dve, 1)
                dve.wait_ge(fin_dve, k)

            dve.wait_ge(bank_read, (2 * HEADS + 1) * BANKS)
            weights(nc.vector, H, 1, link, 0)[0].then_inc(den_made, 1)
            invert(H, 1)
            dve.wait_ge(rden_made, 2 * HEADS)
            rows_of_head(nc.vector, H, 1, link, 2)[0].then_inc(head_out, 1)
            dve.wait_ge(head_out, 2 * HEADS + 2)
            statistics(1)
            scales(1)
            dve.wait_ge(gb_in, 32)
            dve.wait_ge(o_xbeta, NOG)
            for n in VECTOR_GROUPS:
                for B in range(n * OG, (n + 1) * OG):
                    last = nc.vector.scalar_tensor_tensor(out=hx[:, B, 0:D], in0=hx[:, B, 0:D],
                                                          scalar=mv[:, B, 0:1], in1=gam[:, :],
                                                          op0=ALU.subtract, op1=ALU.mult)
                last.then_inc(o_gam_dve, 1)
                dve.wait_ge(o_gam_dve, n + 1 - NOG // 2)
                for B in range(n * OG, (n + 1) * OG):
                    to = o_x1_rows(n)[:, B - n * OG, :]
                    last = nc.vector.scalar_tensor_tensor(out=to, in0=hx[:, B, 0:D],
                                                          scalar=rstd[:, B:B + 1], in1=to,
                                                          op0=ALU.mult, op1=ALU.add)
                last.then_inc(o_made_dve, 1)
            for n in SHARED_GROUPS:
                dve.wait_ge(o_norm, NOG // 2 + 1 + SHARED_GROUPS.index(n) + len(POOL_GROUPS))
                nc.vector.tensor_tensor(o_rows(n), o_rows(n), gam[:, :].unsqueeze(1).to_broadcast([P, OG, D]),
                                        ALU.mult).then_inc(o_gam_dve, 1)
                dve.wait_ge(o_gam_dve, n + 1 - NOG // 2)
                nc.vector.tensor_tensor(o_x1_rows(n), o_rows(n), o_x1_rows(n), ALU.add).then_inc(o_made_dve, 1)

        @block.tensor
        def _(pe):
            pe.wait_ge(consts, 6)

            def flip(t, u, rows_of, read):
                if t < NT // 2:
                    pe.wait_ge(cent_made, 2 * (t + 1))
                elif t < NT:
                    pe.wait_ge(cent_act, t + 1 - NT // 2)
                else:
                    pe.wait_ge(cent_made, t + 1)
                if read > 0:
                    pe.wait_ge(hT_made, read)
                for k in range(2):
                    last = nc.tensor.transpose(ps_t2[u][:, k, :], rows_of(k), ident[:, :])
                last.then_inc(cent_T, 1)

            def project(t, u, w, cols):
                pe.wait_ge(hT_made, t + 1)
                for k in range(2):
                    last = nc.tensor.matmul(ps_p2[u][:, k, 0:cols], hT2[u][:, k, :], w[:, 0:cols],
                                            start=True, stop=True)
                last.then_inc(proj_done, 1)

            def column_sums(bank, done):
                nc.tensor.matmul(ps[:, bank * BANK:bank * BANK + D], ones[:, :], colsum[:, :],
                                 start=True, stop=True).then_inc(done, 1)

            def turn(B):
                for hf in range(2):
                    n = 2 * B + hf
                    pe.wait_ge(packed, n + 1)
                    if n >= 2:
                        pe.wait_ge(adj_kept, n - 1)
                    for a in range(NT // 2):
                        last = nc.tensor.transpose(ps_words[hf][:, a * P:(a + 1) * P],
                                                   words[hf][:, a * P:(a + 1) * P], ident_h[:, :])
                    last.then_inc(transposed, 1)

            pe.wait_ge(wx_made, 1)
            for t in range(NT + 1):
                if t < NT:
                    flip(t, t % 2, lambda k: xin[:, 2 * t + k, :], t - 1)
                if t > 0:
                    if t > 2:
                        pe.wait_ge(h0_made, t - 2)
                    project(t - 1, (t - 1) % 2, wx0, E0)
                if t == 10:
                    turn(0)
            turn(1)
            pe.wait_ge(max_part, 1)
            nc.tensor.matmul(ps[0:1, 6 * BANK:6 * BANK + P], small[:, 0:1], ident[:, :],
                             start=True, stop=True).then_inc(max_row, 1)
            pe.wait_ge(max_one, 1)
            nc.tensor.matmul(ps[:, 7 * BANK:7 * BANK + 1], ones[0:1, :], small[0:1, 2:3],
                             start=True, stop=True).then_inc(max_all, 1)
            pe.wait_ge(colsum_steps, NB + 1)
            column_sums(3, hsum_done)

            def aggregate(B):
                s = B // 2
                pe.wait_ge(adj_kept, 2 * B + 2)
                if B % 2 == 0 and s >= 2:
                    pe.wait_ge(l0_read, s - 1)
                for J in range(NB):
                    if B == 0 and J % CH == 0:
                        pe.wait_ge(v0_cast, V0_COUNT[J // CH, 2])
                    last = nc.tensor.matmul(ps_l0[s % 2][B % 2], adj_f8[:, J // 2, B * P:(B + 1) * P, J % 2],
                                            v0[:, J, :], start=(J == 0), stop=(J == NB - 1))
                last.then_inc(l0_done, 1)

            def project_rows(s):
                if s >= 1:
                    pe.wait_ge(h1_made, 2 * s)
                else:
                    pe.wait_ge(h0_made, NT)
                project(NT + s, 0, wx1, E1)

            def turn_si(g):
                pe.wait_ge(si_flat_made, g + 1)
                pe.wait_ge(adj_kept, 4 * NT)
                nc.tensor.transpose(ps_si[g], si_flat[g], ident[:, :]).then_inc(si_T, 1)

            for t in range(NT + 3):
                s = t - 3
                if 0 < t < NT:
                    turn(2 * t)
                if s >= 0:
                    flip(NT + s, 0, lambda k: cent[:, k, :], NT + s)
                if t == NT:
                    project_rows(s)
                    turn_si(0)
                if 1 <= t <= NT:
                    aggregate(2 * t - 1)
                if 0 < t < NT:
                    turn(2 * t + 1)
                if s >= 0 and t != NT:
                    project_rows(s)
                if t == 0:
                    pe.wait_ge(one_made, 2)
                    pe.wait_ge(hsum_read, 1)
                if t < NT:
                    aggregate(2 * t)

            pe.wait_ge(tr_max, 1)
            nc.tensor.matmul(ps[0:HEADS, 6 * BANK:6 * BANK + P], max4[:, :], ident[:, :],
                             start=True, stop=True).then_inc(tr_pe, 1)
            turn_si(1)
            pe.wait_ge(tr_diag, 1)
            nc.tensor.matmul(ps[:, 7 * BANK:7 * BANK + HEADS], ones[0:HEADS, :], diag4[:, :],
                             start=True, stop=True).then_inc(tr_pe, 1)
            pe.wait_ge(colsum_steps, 2 * NB + 2)
            for k, grants in enumerate((q_used, rest_used)):
                at = 5 * BANK + k * (D // 2)
                nc.tensor.matmul(ps[:, at:at + D // 2], ones[:, :], colsum[:, k * (D // 2):(k + 1) * (D // 2)],
                                 start=True, stop=True).then_inc(grants, 2)

            pe.wait_ge(siT_made, 1)
            def multiply(h, g, jj, b, k, p, n, first, final):
                bank = n // 2
                if first and k == 0 and p == 0 and n % 2 == 0:
                    wait_value(pe, bank_read, h * (2 * BANKS) + g * BANKS + bank + 1)
                at = (n % 2) * 2 * W1 + b * W1
                ins = nc.tensor.matmul(
                    ps_acc[:, bank, at:at + W1], q_f8[k][b][:, n * P:(n + 1) * P, p],
                    v1[:, 2 * (2 * jj + k) + p, b, :],
                    start=(first and k == 0 and p == 0 and n % 2 == 0),
                    stop=(final and k == 1 and p == 1 and n % 2 == 1),
                    skip_group_check=True)
                if p == 1 and n == GB - 1:
                    ins.then_inc(rest_used if b else q_used, 1)
                elif final and k == 1 and p == 1 and n % 2 == 1:
                    ins.then_inc(bank_done, 1)

            with pe.Fori(0, HEADS) as h:
                for g in range(2):
                    for jj in range(NU // 2):
                        u = h * (2 * NU) + g * NU + 2 * jj
                        if g == 0:
                            wait_value(pe, v1_made, h * NCH + jj + 1)
                        for b, ready in enumerate((q_made, rest_made)):
                            first = jj == 0 and b == 0
                            final = jj == NU // 2 - 1 and b == 1
                            if first or final:
                                wait_value(pe, ready, u + 4)
                                for n in range(GB):
                                    for k in range(2):
                                        for p in range(2):
                                            multiply(h, g, jj, b, k, p, n, first, final)
                            else:
                                for k in range(2):
                                    wait_value(pe, ready, u + k + 3)
                                    for p in range(2):
                                        for n in range(GB):
                                            multiply(h, g, jj, b, k, p, n, first, final)


_INS = ['x', 'adj', 'L0_gnn_W_fc', 'L0_gnn_b_fc', 'L0_gnn_w_att', 'L0_gnn_b_att',
        'L1_gnn_W', 'L1_gnn_a', 'L1_gnn_gamma', 'L1_gnn_beta']
_OUTS = [((4096, 128), 'float32')]


def kernel(**inputs):
    import numpy as _np
    import concourse.bacc as _bacc
    from concourse import mybir as _mybir
    from concourse.bass_utils import run_bass_kernel_spmd as _run

    nc = _bacc.Bacc("TRN2", target_bir_lowering=False, num_devices=1, dynamic_dma_scratch_size=2048)
    arrays, args = {}, []
    for name in _INS:
        a = _np.ascontiguousarray(inputs[name])
        if name == 'L0_gnn_b_att':
            a = a.reshape(1)
        arrays[f"in_{name}_dram"] = a
        args.append(nc.dram_tensor(f"in_{name}_dram", a.shape, _mybir.dt.from_np(a.dtype), kind="ExternalInput").ap())
    for i, (shape, dtype) in enumerate(_OUTS):
        dt = _mybir.dt.from_np(_np.dtype(dtype))
        args.append(nc.dram_tensor(f"out_{i}_dram", shape, dt, kind="ExternalOutput").ap())
    gnn_two_layers(nc, *args)
    nc.compile()
    r = _run(nc, [arrays], core_ids=[0])
    return r.results[0]["out_0_dram"]
```
